# Optimizing a Trainium2 kernel written in Bass

```python
import numpy as np
import jax
import jax.numpy as jnp

def _softmax(x, axis=-1):
    return jax.nn.softmax(x, axis=axis)

def _gelu(x):
    return jax.nn.gelu(x, approximate=True)

def _silu(x):
    return jax.nn.silu(x)

def _sigmoid(x):
    return jax.nn.sigmoid(x)

def _layernorm(x, axis=-1, eps=1e-05):
    m = jnp.mean(x, axis=axis, keepdims=True)
    v = jnp.var(x, axis=axis, keepdims=True)
    return (x - m) / jnp.sqrt(v + eps)

def _scatter_add(tgt, idx, src, axis=0):
    return tgt.at[idx].add(src)

def _segment_sum(src, seg, n):
    return jax.ops.segment_sum(src, seg, n)
kernel_name = 'mk_prb_d1_jaxref_r8_5bf8eb'

def setup_inputs(seed: int=0):
    np.random.seed(seed)
    _w = jnp.asarray

    def _L0_attn_setup():
        import jax, jax.numpy as jnp
        import numpy as np
        import math
        HIDDEN = 256
        NUM_HEADS = 16
        HEAD_SIZE = HIDDEN // NUM_HEADS
        BATCH = 2
        SEQ = 256
        key = jax.random.key(seed)
        k_x, k_wq, k_bq, k_wo, k_bo = jax.random.split(key, 5)
        scale_in = 1.0 / math.sqrt(HIDDEN)
        return {'x': jax.random.normal(k_x, (BATCH, SEQ, HIDDEN), dtype=jnp.float32), 'Wqkv': jax.random.normal(k_wq, (HIDDEN, 3 * HIDDEN), dtype=jnp.float32) * scale_in, 'bqkv': jax.random.normal(k_bq, (3 * HIDDEN,), dtype=jnp.float32) * 0.01, 'Wo': jax.random.normal(k_wo, (HIDDEN, HIDDEN), dtype=jnp.float32) * scale_in, 'bo': jax.random.normal(k_bo, (HIDDEN,), dtype=jnp.float32) * 0.01}
    _L0_attn_in = _L0_attn_setup()

    def _L0_ffn_setup():
        import jax, jax.numpy as jnp
        import numpy as np
        _FP8_DTYPE = jnp.float8_e4m3fn
        _FP8_MAX = 448.0
        key = jax.random.key(seed)
        k_x, k_w = jax.random.split(key)
        B, S, IN, OUT = (2, 1024, 256, 256)
        x = jax.random.normal(k_x, (B, S, IN), dtype=jnp.float32)
        w_f32 = jax.random.normal(k_w, (OUT, IN), dtype=jnp.float32) * 0.02
        weight = w_f32.astype(_FP8_DTYPE)
        weight_scale = jnp.asarray(1.5, dtype=jnp.float32)
        input_scale = jnp.asarray(0.75, dtype=jnp.bfloat16)
        return {'x': x, 'weight': weight, 'weight_scale': weight_scale, 'input_scale': input_scale}
    _L0_ffn_in = _L0_ffn_setup()
    _d = {'L0_attn_x': _L0_attn_in['x'], 'L0_attn_Wqkv': _L0_attn_in['Wqkv'], 'L0_attn_bqkv': _L0_attn_in['bqkv'], 'L0_attn_Wo': _L0_attn_in['Wo'], 'L0_attn_bo': _L0_attn_in['bo'], 'L0_ffn_weight': _L0_ffn_in['weight'], 'L0_ffn_weight_scale': _L0_ffn_in['weight_scale'], 'L0_ffn_input_scale': _L0_ffn_in['input_scale']}
    _x0 = _d['L0_attn_x']
    _d['L0_attn_x'] = jax.random.normal(jax.random.fold_in(jax.random.key(seed), 1), (8, 256, 256), dtype=_x0.dtype)
    del _x0
    return _d

def reference(L0_attn_x, L0_attn_Wqkv, L0_attn_bqkv, L0_attn_Wo, L0_attn_bo, L0_ffn_weight, L0_ffn_weight_scale, L0_ffn_input_scale):

    def _L0_attn_ref(x, Wqkv, bqkv, Wo, bo):
        import jax, jax.numpy as jnp
        import numpy as np
        import math
        HIDDEN = 256
        NUM_HEADS = 16
        HEAD_SIZE = HIDDEN // NUM_HEADS
        BATCH = 2
        SEQ = 256
        b, s, _ = x.shape
        kqv = x @ Wqkv + bqkv
        kqv = kqv.reshape(b, s, 3, NUM_HEADS, HEAD_SIZE)
        q = kqv[:, :, 0]
        k = kqv[:, :, 1]
        v = kqv[:, :, 2]
        scores = jnp.einsum('bsnh,btnh->bnst', k, q) / math.sqrt(HEAD_SIZE)
        ones = jnp.ones_like(scores)
        scores = jnp.triu(scores) + -10000.0 * jnp.tril(ones, k=-1)
        attn = jax.nn.softmax(scores, axis=2)
        out = jnp.einsum('bnkq,bknh->bqnh', attn, v)
        out = out.reshape(b, s, NUM_HEADS * HEAD_SIZE)
        return out @ Wo + bo

    def _L0_ffn_ref(x, weight, weight_scale, input_scale):
        import jax, jax.numpy as jnp
        import numpy as np
        _FP8_DTYPE = jnp.float8_e4m3fn
        _FP8_MAX = 448.0
        orig_dtype = x.dtype
        w = weight.astype(orig_dtype) * weight_scale.astype(orig_dtype)
        s_f32 = input_scale.astype(jnp.float32)
        x_scaled = x.astype(jnp.float32) / s_f32
        x_fp8 = jnp.clip(x_scaled, -_FP8_MAX, _FP8_MAX).astype(_FP8_DTYPE)
        x_qdq = x_fp8.astype(orig_dtype) * s_f32.astype(orig_dtype)
        return jnp.einsum('bsi,oi->bso', x_qdq, w)
    x = L0_attn_x
    xn = _layernorm(x, axis=-1)
    x = x + _L0_attn_ref(xn, L0_attn_Wqkv, L0_attn_bqkv, L0_attn_Wo, L0_attn_bo) + _L0_ffn_ref(xn, L0_ffn_weight, L0_ffn_weight_scale, L0_ffn_input_scale)
    return x

_drawn_inputs = setup_inputs


def setup_inputs(seed=0):
    import zlib

    import numpy as np

    out = dict(_drawn_inputs(seed))
    spreads = {}
    factors = {'L0_attn_bqkv': 5.51, 'L0_attn_bo': 6.672}
    for name, (base, spread) in spreads.items():
        noise = np.random.default_rng([zlib.crc32(name.encode()), seed]).standard_normal(out[name].shape)
        drawn = base * np.exp(spread * noise) if base else spread * noise
        out[name] = jnp.asarray(drawn.astype(out[name].dtype))
    for name, factor in factors.items():
        out[name] = (out[name] * factor).astype(out[name].dtype)
    return out
```

```python
from contextlib import ExitStack

import concourse.bass as bass
from concourse import mybir

ALU = mybir.AluOpType
ACT = mybir.ActivationFunctionType
AX_X = mybir.AxisListType.X
BF16 = mybir.dt.bfloat16
FP16 = mybir.dt.float16
F32 = mybir.dt.float32
I32 = mybir.dt.int32
U8 = mybir.dt.uint8
U16 = mybir.dt.uint16

P = 128
B = 8
S = 256
D = 256
H = 16
HD = D // H
TB = S // P
KT = D // P
HALF = H // 2
SLOTS = 6
EPS = 1e-5
SCALE = HD ** -0.5
MASKED = -10000.0 / SCALE
FP8_MAX = 448.0

PARTS = 3
Q_ORDER = (0, 1, 2, 0, 1, 0)
K_ORDER = (0, 0, 0, 1, 1, 2)
PROD = len(Q_ORDER) * HD
Q_READ = 112
ROW_MAX = PROD
ROW_MASK = PROD + PARTS
MB = 5
MASK_ROWS = -(-P // MB)
K_SOFT = PROD + PARTS
K_MAX = ROW_MASK + MASK_ROWS
G = 2.0 ** 24
MASK_C = 16.0
NVC = HD + 1

USES = {
    "A": [("norm_o0", -1), ("max_h1", 0), ("k", 2), ("o1", -1), ("ffn", 0), ("norm_o1", -1), ("proj", -1)],
    "B": [("xT", 2), ("q", 2), ("suffix1", -1), ("v", 1), ("suffix0", 0), ("max_h0", 1), ("o0", 0)],
}
FIRST, LAST = -2, B
LOOP = range(2, 6)


class Step:

    def __init__(self, n, like):
        self.n, self.like, self.par = n, like, like % 2

    def has(self, off):
        return 0 <= self.like + off < B

    def use_before(self, bank, name):
        order = [who for who, _ in USES[bank]]
        at, like, n = order.index(name), self.like, self.n
        while like >= FIRST:
            for who, off in reversed(USES[bank][:at]):
                if 0 <= like + off < B:
                    return who, n + off
            at, like, n = len(order), like - 1, n - 1
        return None


def all_steps(eng, run):
    for n in range(FIRST, LOOP.start):
        run(Step(n, n))
    with eng.Fori(0, len(LOOP) // 2) as turn:
        n = turn * 2 + LOOP.start
        run(Step(n, LOOP.start))
        run(Step(n + 1, LOOP.start + 1))
    for n in range(LOOP.stop, LAST + 1):
        run(Step(n, n))


def wait(eng, sem, value, passed=None):
    if not isinstance(value, int) or value > 0:
        eng.wait_ge(sem, value)
        if not isinstance(value, int) and passed is not None:
            eng.sem_inc(passed, 1)


def build(nc, x, wqkv, bqkv, wo, bo, w8, w8_scale, in_scale, out):
    ctx = ExitStack()
    with ctx:
        def sb(name, shape, dt=F32):
            return ctx.enter_context(nc.sbuf_tensor(name, shape, dt))

        def psum(name, shape, dt=F32):
            return ctx.enter_context(nc.psum_tensor(name, shape, dt))

        def sem(name):
            return ctx.enter_context(nc.semaphore(name))

        ident = sb("ident", [P, P])
        ident_bf = sb("ident_bf", [P, P], BF16)
        later = sb("later", [P, P])
        ones = sb("ones", [P, P])
        mask_q = sb("mask_q", [MASK_ROWS, P], BF16)
        mask_k = sb("mask_k", [MASK_ROWS, P], BF16)
        zero_rows = sb("zero_rows", [PARTS, H * S], BF16)
        neg_floor = sb("neg_floor", [P, TB, HALF])
        wqkv_sb = sb("wqkv_sb", [P, KT, 3 * D])
        wqk_sb = sb("wqk_sb", [P, KT, 2 * D])
        wo_sb = sb("wo_sb", [P, KT, D])
        bqk_row = sb("bqk_row", [2 * KT, P])
        bqk_ordered = sb("bqk_ordered", [2 * KT, P])
        bqk_col = sb("bqk_col", [P, 2 * KT])
        bv_all = sb("bv_all", [P, D])
        bo_all = sb("bo_all", [P, D])
        w8_raw = sb("w8_raw", [P, KT, D], U8)
        w8_wide = sb("w8_wide", [P, KT, D], U16)
        w8_mag = sb("w8_mag", [P, KT, D], U16)
        w8_sign = sb("w8_sign", [P, KT, D], U16)
        w8_bits = sb("w8_bits", [P, KT, D], U16)
        w8_bf = sb("w8_bf", [P, KT, D], BF16)
        w8T = sb("w8T", [P, KT, D], BF16)
        in_scale_bf = sb("in_scale_bf", [P, 1], BF16)
        in_scale_f = sb("in_scale_f", [P, 1])
        w8_scale_f = sb("w8_scale_f", [P, 1])
        inv_in_scale = sb("inv_in_scale", [P, 1])
        ffn_scale = sb("ffn_scale", [P, 1])

        NT = B * TB
        x_all = sb("x_all", [P, NT, D])
        stats = sb("stats", [P, NT, 6])
        mean_var = sb("mean_var", [P, NT, 2])
        var_eps = sb("var_eps", [P, NT])
        std = sb("std", [P, NT])
        rstd0 = sb("rstd0", [P, NT])
        rstd_sq = sb("rstd_sq", [P, NT])
        rstd_e = sb("rstd_e", [P, NT])
        rstd_f = sb("rstd_f", [P, NT])
        rstd = sb("rstd", [P, NT])
        xn = sb("xn", [P, 2, TB, D])

        xT = sb("xT", [P, 2, KT, S])
        x_over = sb("x_over", [P, KT, S])
        x_clip = sb("x_clip", [P, KT, S])
        x_exp = sb("x_exp", [P, KT, S])
        x_big = sb("x_big", [P, KT, S])
        x_sum = sb("x_sum", [P, KT, S])
        xq = sb("xq", [P, 2, KT, S], BF16)
        parts = {qk: sb(f"{qk}_parts", [P, 2, PARTS, KT, S], BF16) for qk in "qk"}
        rest = {qk: sb(f"{qk}_rest", [P, KT, S]) for qk in "qk"}
        q_stack = sb("q_stack", [P, 2, H, S], BF16)
        k_stack = sb("k_stack", [P, 2, H, S], BF16)
        v_sb = sb("v_sb", [P, 2, TB, H, 32])
        row_max = sb("row_max", [P, 2, TB, HALF])
        neg_max = sb("neg_max", [P, 2, TB, HALF])
        neg_r1 = sb("neg_r1", [P, 2, TB, HALF])
        neg_parts = sb("neg_parts", [P, 2, TB, PARTS, HALF], BF16)
        e_arg = sb("e_arg", [P, 2, TB, HALF])
        e_sb = sb("e_sb", [P, 2, 2, TB, HALF])
        max_rows = sb("max_rows", [PARTS * HALF, 2, S], BF16)
        probs = sb("probs", [P, 2, 1024])
        o_raw = sb("o_raw", [P, 2, 2, S])
        o_masked = sb("o_masked", [P, 2, H, NVC])
        o_sum = sb("o_sum", [P, 2, H, NVC])
        o_den = sb("o_den", [P, 2, H])
        o_tok = sb("o_tok", [P, 2, TB, P])
        oT = sb("oT", [P, KT, S])
        xb = sb("xb", [P, TB, D])
        y1 = sb("y1", [P, 2, TB, D])
        y = sb("y", [P, 2, TB, D])

        scratch = {qk: nc.dram_tensor(f"{qk}_scratch", (2, rows, HALF, 2, S), BF16, kind="Internal").ap()
                   for qk, rows in (("q", Q_READ), ("k", PROD))}
        ps1 = psum("ps1", [P, 1024])
        ps2 = psum("ps2", [P, 1024])
        pso = psum("pso", [P, 2, 2, S])
        bank = {"A": psum("bankA", [P, 512]), "B": psum("bankB", [P, 512])}

        x0_landed, x_landed = sem("x0_landed"), sem("x_landed")
        w_landed, wo_landed, small_landed = sem("w_landed"), sem("wo_landed"), sem("small_landed")
        passed = sem("passed")
        const_ready, pool_chain = sem("const_ready"), sem("pool_chain")
        ones_ready = sem("ones_ready")
        w_ordered = sem("w_ordered")
        mask_landed = sem("mask_landed")
        init_dve = sem("init_dve")
        std_ready = sem("std_ready")
        w8_chain, w8_mm, w8T_ready = sem("w8_chain"), sem("w8_mm"), sem("w8T_ready")
        scales_ready = sem("scales_ready")
        xn_ready, xT_mm, xT_ready = sem("xn_ready"), sem("xT_mm"), sem("xT_ready")
        q_mm, k_mm, v_mm = sem("q_mm"), sem("k_mm"), sem("v_mm")
        part1_ready, rest_ready = sem("part1_ready"), sem("rest_ready")
        part2_ready, split_ready = sem("part2_ready"), sem("split_ready")
        spilled = [sem(f"{qk}_spilled") for qk in "qk"]
        stack_landed = [sem(f"stack_landed{h}") for h in range(2)]
        v_ready = sem("v_ready")
        ph1_mm, max_done = sem("ph1_mm"), sem("max_done")
        neg_step, max_mm, max_rows_ready = sem("neg_step"), sem("max_mm"), sem("max_rows_ready")
        max_landed = [sem(f"max_landed{h}") for h in range(2)]
        e_ready = sem("e_ready")
        ph2_mm, exp_done, causal_done, pv_mm = sem("ph2_mm"), sem("exp_done"), sem("causal_done"), sem("pv_mm")
        o_raw_ready, o_mm, suffix_mm = sem("o_raw_ready"), sem("o_mm"), sem("suffix_mm")
        masked_ready, norm_step = sem("masked_ready"), sem("norm_step")
        oT_mm, oT_ready = sem("oT_mm"), sem("oT_ready")
        quant_dve, quant_pool = sem("quant_dve"), sem("quant_pool")
        ffn_mm, xb_ready, y1_ready = sem("ffn_mm"), sem("xb_ready"), sem("y1_ready")
        proj_mm, y_ready = sem("proj_mm"), sem("y_ready")
        out_landed = [sem(f"out_landed{p}") for p in range(2)]
        read = {"xT": (xT_ready, 1, 1), "q": (rest_ready, 2, 1), "k": (rest_ready, 2, 2),
                "v": (v_ready, 1, 1), "max_h0": (max_rows_ready, 2, 1), "max_h1": (max_rows_ready, 2, 2),
                "suffix0": (masked_ready, 2, 1), "suffix1": (masked_ready, 2, 2),
                "o0": (norm_step, 6, 1), "o1": (norm_step, 6, 4),
                "norm_o0": (oT_ready, 2, 1), "norm_o1": (oT_ready, 2, 2),
                "ffn": (y1_ready, 1, 1), "proj": (y_ready, 1, 1)}

        STACK_DMAS = 2
        SPILL_DMAS = 3
        CONSTS = 4

        x_tok = x.rearrange("b (t p) d -> p (b t) d", p=P)
        block = ctx.enter_context(nc.Block())

        @block.sync
        def _(sp):
            for par in range(2):
                sp.sem_inc(out_landed[par], 16)
            sp.dma_start(x_all[:, 0:TB, :], x_tok[:, 0:TB, :]).then_inc(x0_landed, 16)
            sp.dma_start(wqkv_sb[:], wqkv.rearrange("(k p) n -> p k n", p=P)).then_inc(w_landed, 16)
            for t, src in ((bqk_row[:], bqkv[0:2 * D].rearrange("(m p) -> m p", p=P)),
                           (bv_all[:], bqkv[2 * D:3 * D].partition_broadcast(P)),
                           (bo_all[:], bo.partition_broadcast(P)),
                           (w8_raw[:], w8.bitcast(U8).rearrange("(k p) n -> p k n", p=P)),
                           (in_scale_bf[:], in_scale.partition_broadcast(P)),
                           (w8_scale_f[:], w8_scale.partition_broadcast(P))):
                sp.dma_start(t, src).then_inc(small_landed, 16)
            sp.dma_start(x_all[:, TB:, :], x_tok[:, TB:, :]).then_inc(x_landed, 16)
            sp.dma_start(wo_sb[:], wo.rearrange("(k p) n -> p k n", p=P)).then_inc(wo_landed, 16)
            sp.wait_ge(const_ready, CONSTS)
            for stack, rows in ((q_stack, mask_q), (k_stack, mask_k)):
                for par in range(2):
                    dst = stack[ROW_MASK:K_MAX, par].rearrange("r h (t p) -> r (h t) p", p=P)
                    sp.dma_start(dst, rows[:].unsqueeze(1).to_broadcast([MASK_ROWS, H * TB, P])).then_inc(mask_landed, 16)
            for par in range(2):
                again = Q_READ - ROW_MASK
                sp.dma_start(scratch["q"][par, ROW_MASK:Q_READ].rearrange("r h k (t p) -> r (h k t) p", p=P),
                             mask_q[0:again].unsqueeze(1).to_broadcast([again, H * TB, P])).then_inc(mask_landed, 16)
                sp.dma_start(scratch["q"][par, ROW_MAX:ROW_MASK].rearrange("r h k t -> r (h k t)"),
                             zero_rows[:]).then_inc(mask_landed, 16)
            sp.wait_ge(mask_landed, 8 * 16)

            def spill(b, par, qk):
                j = "qk".index(qk)
                wait(sp, split_ready, 2 * b + j + 1, passed)
                for half in range(2):
                    wait(sp, stack_landed[half], 16 * STACK_DMAS * (b - 1), passed)
                row = 0
                for parts_of in ((0, 1, 2), (0, 1), (0,)) if qk == "q" else ((0, 0, 0), (1, 1), (2,)):
                    c = len(parts_of)
                    src = parts[qk][:, par, parts_of[0]:parts_of[-1] + 1].rearrange("p i k t -> p i (k t)")
                    if qk == "k":
                        src = src.to_broadcast([P, c, KT * S])
                    sp.dma_start(scratch[qk][par, row:row + HD * c].rearrange("(i d) h k t -> (d h) i (k t)", i=c),
                                 src).then_inc(spilled[j], 16)
                    row += HD * c

            def stack(b, par, half):
                wait(sp, ph2_mm, SLOTS * (b - 2) + 3 * half + 3, passed)
                heads = slice(HALF * half, HALF * half + HALF)
                for j, (stack_sb, qk, rows) in enumerate(((q_stack, "q", Q_READ), (k_stack, "k", PROD))):
                    wait(sp, spilled[j], 16 * SPILL_DMAS * (b + 1), passed)
                    sp.dma_start(stack_sb[0:rows, par, heads, :],
                                 scratch[qk][par, :, :, half, :]).then_inc(stack_landed[half], 16)

            def max_to_stack(b, par, half):
                wait(sp, max_rows_ready, 2 * b + half + 1, passed)
                for r in range(PARTS):
                    sp.dma_start(q_stack[ROW_MAX + r:ROW_MAX + r + 1, par, HALF * half:HALF * half + HALF, :],
                                 max_rows[HALF * r:HALF * r + HALF, half, :]).then_inc(max_landed[half], 16)

            def run(st):
                n, p = st.n, st.par
                if st.has(0):
                    max_to_stack(n, p, 1)
                if st.has(2):
                    spill(n + 2, p, "q")
                    spill(n + 2, p, "k")
                    stack(n + 2, p, 0)
                if st.has(1):
                    max_to_stack(n + 1, 1 - p, 0)
                if st.has(-1):
                    wait(sp, y_ready, n, passed)
                    sp.dma_start(out[bass.ds(n - 1, 1)].rearrange("b (t p) d -> p (b t) d", p=P),
                                 y[:, 1 - p]).then_inc(out_landed[1 - p], 16)
                if st.has(2):
                    stack(n + 2, p, 1)

            all_steps(sp, run)
            for par in range(2):
                sp.wait_ge(out_landed[par], 16 + 16 * B // 2)

        @block.gpsimd
        def _(pool):
            steps = [0]

            def link(ins):
                steps[0] += 1
                ins.then_inc(pool_chain, 1)
                pool.wait_ge(pool_chain, steps[0])

            pool.memset(ident[:], 0.0)
            pool.memset(later[:], 1.0)
            pool.memset(ones[:], 1.0)
            pool.memset(mask_q[:], 0.0)
            link(pool.memset(mask_k[:], 0.0))
            link(pool.affine_select(out=ident[:], in_=ident[:], compare_op=ALU.not_equal, fill=1.0,
                                    base=0, pattern=[[-1, P]], channel_multiplier=1))
            pool.tensor_copy(ident_bf[:], ident[:]).then_inc(const_ready, 1)
            pool.affine_select(out=later[:], in_=later[:], compare_op=ALU.is_gt, fill=0.0,
                               base=0, pattern=[[-1, P]], channel_multiplier=1).then_inc(const_ready, 1)
            link(pool.affine_select(out=mask_q[:], in_=mask_q[:], compare_op=ALU.is_ge, fill=G,
                                    base=0, pattern=[[1, P]], channel_multiplier=-MB))
            for j in range(MB):
                link(pool.affine_select(out=mask_q[:], in_=mask_q[:], compare_op=ALU.not_equal, fill=G ** -j,
                                        base=-j, pattern=[[1, P]], channel_multiplier=-MB))
                link(pool.affine_select(out=mask_k[:], in_=mask_k[:], compare_op=ALU.not_equal,
                                        fill=-MASK_C * G ** j,
                                        base=-j, pattern=[[1, P]], channel_multiplier=-MB))
            link(pool.memset(neg_floor[:], -MASKED))
            pool.affine_select(out=neg_floor[:, TB - 1], in_=neg_floor[:, TB - 1], compare_op=ALU.not_equal,
                               fill=3.0e38, base=-(P - 1), pattern=[[0, HALF]],
                               channel_multiplier=1).then_inc(const_ready, 1)
            pool.wait_ge(const_ready, CONSTS - 1)
            pool.memset(zero_rows[:], 0.0).then_inc(const_ready, 1)
            pool.wait_ge(const_ready, CONSTS)
            pool.memset(k_stack[ROW_MAX:ROW_MASK].bitcast(I32), 0x3F803F80).then_inc(ones_ready, 1)
            pool.wait_ge(ones_ready, 1)

            def causal(b, i):
                c = SLOTS * b + i
                wait(pool, exp_done, c + 1, passed)
                pr = probs[:, i % 2, :]
                if i % 3 < 2:
                    v, heads = pr.rearrange("p (h t) -> p h t", h=4)[:, :, 0:P], 4
                else:
                    v, heads = pr.rearrange("p (h t) -> p h t", h=HALF), HALF
                pool.affine_select(out=v, in_=v, compare_op=ALU.is_ge, fill=0.0, base=0,
                                   pattern=[[0, heads], [1, P]], channel_multiplier=-1).then_inc(causal_done, 1)

            def split(b, par, qk):
                j = "qk".index(qk)
                pt, r = parts[qk], rest[qk]
                wait(pool, rest_ready, 2 * b + j + 1, passed)
                pool.tensor_scalar(pt[:, par, 1], r[:], 1.0, 1.0, ALU.mult, ALU.mult).then_inc(part2_ready, 1)
                wait(pool, part2_ready, 2 * b + j + 1, passed)
                pool.tensor_tensor(pt[:, par, 2], r[:], pt[:, par, 1], ALU.subtract).then_inc(split_ready, 1)

            def run(st):
                n, p = st.n, st.par
                if st.has(0):
                    causal(n, 0)
                    causal(n, 1)
                if st.has(2):
                    split(n + 2, p, "q")
                if st.has(0):
                    causal(n, 2)
                    wait(pool, y1_ready, n, passed)
                    if st.like == 0:
                        pool.wait_ge(small_landed, 6 * 16)
                        wait(pool, x0_landed, 16, passed)
                        wait(pool, x_landed, 16, passed)
                    pool.tensor_tensor(xb[:], x_all[:, bass.ds(TB * n, TB), :],
                                       bo_all[:].unsqueeze(1).to_broadcast([P, TB, D]),
                                       ALU.add).then_inc(xb_ready, 1)
                if st.has(2):
                    split(n + 2, p, "k")
                if st.has(0):
                    causal(n, 3)
                if st.has(0):
                    causal(n, 4)
                if st.has(2):
                    b = n + 2
                    wait(pool, quant_dve, 4 * b + 4, passed)
                    pool.tensor_tensor(x_sum[:], x_clip[:], x_big[:], ALU.add).then_inc(quant_pool, 1)
                    wait(pool, quant_pool, 2 * b + 1, passed)
                    wait(pool, ffn_mm, b - 1, passed)
                    pool.tensor_tensor(xq[:, p], x_sum[:], x_big[:], ALU.subtract).then_inc(quant_pool, 1)
                if st.has(0):
                    causal(n, 5)

            all_steps(pool, run)

        @block.scalar
        def _(act):
            act.wait_ge(w_landed, 16)
            for k in range(KT):
                ins = act.activation(wqk_sb[:, k].rearrange("p (m d h) -> p m d h", m=2 * KT, d=HD),
                                     wqkv_sb[:, k, 0:2 * D].rearrange("p (m h d) -> p m d h", m=2 * KT, d=HD), ACT.Copy)
            ins.then_inc(w_ordered, 1)
            for g in range(2):
                tiles = slice(0, TB) if g == 0 else slice(TB, NT)
                act.wait_ge(init_dve, 2 * g + 1)
                act.activation(std[:, tiles], var_eps[:, tiles], ACT.Sqrt).then_inc(std_ready, 1)

            def exponentials(b, i):
                c = SLOTS * b + i
                act.wait_ge(ph2_mm, c + 1)
                wait(act, pv_mm, c - 1)
                act.activation(probs[:, i % 2, :], ps2[:], ACT.Exp, scale=SCALE).then_inc(exp_done, 1)

            def part1(b, par, qk, bk):
                j = "qk".index(qk)
                act.wait_ge((q_mm, k_mm)[j], b + 1)
                wait(act, spilled[j], 16 * SPILL_DMAS * (b - 1))
                for half in range(2):
                    ins = act.activation(parts[qk][:, par, 0, half, :], bank[bk][:, half * S:half * S + S],
                                         ACT.Identity, bias=bqk_col[:, KT * j + half:KT * j + half + 1])
                ins.then_inc(part1_ready, 1)

            def o_out(b, half):
                c = 2 * b + half
                act.wait_ge(pv_mm, SLOTS * b + 3 * half + 3)
                wait(act, o_mm, c - 1)
                act.activation(o_raw[:, half], pso[:, half], ACT.Copy).then_inc(o_raw_ready, 1)

            def oT_out(b, half, bk):
                c = 2 * b + half
                act.wait_ge(oT_mm, c + 1)
                wait(act, proj_mm, b)
                act.activation(oT[:, half], bank[bk][:, 0:S], ACT.Copy).then_inc(oT_ready, 1)

            def max_out(b, par, half, bk):
                c = 2 * b + half
                act.wait_ge(neg_step, SLOTS * c + 6)
                wait(act, masked_ready, c - 3)
                act.activation(e_sb[:, par, half], e_arg[:, half], ACT.Exp, scale=SCALE).then_inc(e_ready, 1)
                act.wait_ge(max_mm, c + 1)
                wait(act, max_landed[half], 16 * PARTS * b)
                act.activation(max_rows[:, half, :], bank[bk].ap().bitcast(BF16)[0:PARTS * HALF, 0:S],
                               ACT.Copy).then_inc(max_rows_ready, 1)

            def run(st):
                n, p = st.n, st.par
                if st.has(0):
                    exponentials(n, 0)
                if st.has(-1):
                    o_out(n - 1, 1)
                    oT_out(n - 1, 0, "A")
                if st.has(2):
                    b = n + 2
                    act.wait_ge(xT_mm, b + 1)
                    wait(act, v_mm, b - 1)
                    wait(act, quant_dve, 4 * (b - 2) + 1)
                    act.activation(xT[:, p], bank["B"][:].rearrange("p (k s) -> p k s", k=KT), ACT.Copy).then_inc(xT_ready, 1)
                if st.has(0):
                    exponentials(n, 1)
                    max_out(n, p, 1, "A")
                if st.has(2):
                    if st.like == FIRST:
                        act.wait_ge(w8T_ready, 2)
                    part1(n + 2, p, "q", "B")
                if st.has(0):
                    exponentials(n, 2)
                if st.has(2):
                    part1(n + 2, p, "k", "A")
                if st.has(0):
                    exponentials(n, 3)
                    o_out(n, 0)
                    exponentials(n, 4)
                if st.has(-1):
                    oT_out(n - 1, 1, "A")
                if st.has(1):
                    max_out(n + 1, 1 - p, 0, "B")
                if st.has(0):
                    exponentials(n, 5)

            all_steps(act, run)

        @block.vector
        def _(dve):
            steps = [0]

            def link(ins, s=w8_chain):
                steps[0] += 1
                ins.then_inc(s, 1)
                dve.wait_ge(s, steps[0])

            def statistics(g):
                lo, hi = (0, TB) if g == 0 else (TB, NT)
                dve.wait_ge(x0_landed if g == 0 else x_landed, 16)
                for t in range(lo, hi):
                    ins = dve.bn_stats(stats[:, t, :], x_all[:, t, :])
                link(ins)
                for t in range(lo, hi):
                    ins = dve.bn_aggr(mean_var[:, t, :], stats[:, t, :])
                link(ins)
                dve.tensor_scalar(var_eps[:, lo:hi], mean_var[:, lo:hi, 1], EPS, None, ALU.add).then_inc(init_dve, 1)
                dve.wait_ge(std_ready, g + 1)
                link(dve.reciprocal(rstd0[:, lo:hi], std[:, lo:hi]))
                link(dve.tensor_tensor(rstd_sq[:, lo:hi], rstd0[:, lo:hi], rstd0[:, lo:hi], ALU.mult))
                link(dve.tensor_tensor(rstd_e[:, lo:hi], rstd_sq[:, lo:hi], var_eps[:, lo:hi], ALU.mult))
                link(dve.tensor_scalar(rstd_f[:, lo:hi], rstd_e[:, lo:hi], -0.5, 1.5, ALU.mult, ALU.add))
                dve.tensor_tensor(rstd[:, lo:hi], rstd0[:, lo:hi], rstd_f[:, lo:hi], ALU.mult).then_inc(init_dve, 1)
                dve.wait_ge(init_dve, 2 * g + 2)

            def normalise(b, par):
                wait(dve, xT_mm, b - 1)
                for t in range(TB):
                    i = TB * b + t
                    ins = dve.tensor_scalar(xn[:, par, t, :], x_all[:, bass.ds(i, 1), :].rearrange("p t d -> p (t d)"),
                                            mean_var[:, bass.ds(i, 1), 0], rstd[:, bass.ds(i, 1)],
                                            ALU.subtract, ALU.mult)
                ins.then_inc(xn_ready, 1)

            def fp8_weight():
                dve.wait_ge(small_landed, 6 * 16)
                link(dve.tensor_copy(w8_wide[:], w8_raw[:]))
                dve.tensor_scalar(w8_mag[:], w8_wide[:], 0x7F, 7, ALU.bitwise_and, ALU.logical_shift_left)
                link(dve.tensor_scalar(w8_sign[:], w8_wide[:], 0x80, 8, ALU.bitwise_and, ALU.logical_shift_left))
                link(dve.tensor_tensor(w8_bits[:], w8_mag[:], w8_sign[:], ALU.bitwise_or))
                link(dve.tensor_scalar(w8_bf[:], w8_bits[:].bitcast(FP16), 256.0, None, ALU.mult))
                link(dve.tensor_copy(in_scale_f[:], in_scale_bf[:]))
                link(dve.tensor_tensor(ffn_scale[:], in_scale_f[:], w8_scale_f[:], ALU.mult))
                link(dve.tensor_copy(bqk_ordered[:].rearrange("m (d h) -> m d h", d=HD),
                                     bqk_row[:].rearrange("m (h d) -> m d h", d=HD)))
                dve.reciprocal(inv_in_scale[:], in_scale_f[:]).then_inc(scales_ready, 1)

            def maxima(b, i):
                half, j = i // 3, i % 3
                dve.wait_ge(ph1_mm, SLOTS * b + i + 1)
                if j == 0:
                    src, dst = ps1[:].rearrange("p (h s) -> p h s", h=HALF), row_max[:, half, 0, :]
                else:
                    src, dst = ps1[:].rearrange("p (h s) -> p h s", h=4), row_max[:, half, 1, 4 * j - 4:4 * j]
                dve.tensor_reduce(dst, src, AX_X, ALU.max).then_inc(max_done, 1)

            def negate_and_split(b, half):
                c = 2 * b + half
                at = SLOTS * c
                dve.wait_ge(max_done, SLOTS * b + 3 * half + 3)
                wait(dve, e_ready, c - 1)
                dve.scalar_tensor_tensor(out=neg_max[:, half], in0=row_max[:, half], scalar=-1.0,
                                         in1=neg_floor[:], op0=ALU.mult, op1=ALU.min).then_inc(neg_step, 1)
                dve.wait_ge(neg_step, at + 1)
                wait(dve, max_mm, c - 1)
                dve.tensor_copy(neg_parts[:, half, :, 0, :], neg_max[:, half]).then_inc(neg_step, 1)
                dve.tensor_scalar(e_arg[:, half], neg_max[:, half], MASKED, 0.0, ALU.add, ALU.min).then_inc(neg_step, 1)
                dve.wait_ge(neg_step, at + 2)
                dve.tensor_tensor(neg_r1[:, half], neg_max[:, half], neg_parts[:, half, :, 0, :],
                                  ALU.subtract).then_inc(neg_step, 1)
                dve.wait_ge(neg_step, at + 4)
                dve.tensor_copy(neg_parts[:, half, :, 1, :], neg_r1[:, half]).then_inc(neg_step, 1)
                dve.wait_ge(neg_step, at + 5)
                dve.tensor_tensor(neg_parts[:, half, :, 2, :], neg_r1[:, half], neg_parts[:, half, :, 1, :],
                                  ALU.subtract).then_inc(neg_step, 1)

            def rest1(b, par, qk, bk):
                j = "qk".index(qk)
                dve.wait_ge(part1_ready, 2 * b + j + 1)
                wait(dve, split_ready, 2 * (b - 1) + j + 1)
                for half in range(2):
                    ins = dve.scalar_tensor_tensor(out=rest[qk][:, half, :], in0=bank[bk][:, half * S:half * S + S],
                                                   scalar=bqk_col[:, KT * j + half:KT * j + half + 1],
                                                   in1=parts[qk][:, par, 0, half, :], op0=ALU.add, op1=ALU.subtract)
                ins.then_inc(rest_ready, 1)

            def masked_part(b, par, half, bk):
                c = 2 * b + half
                dve.wait_ge(suffix_mm, c + 1)
                dve.wait_ge(e_ready, c + 1)
                wait(dve, norm_step, 3 * (c - 2) + 1)
                dve.tensor_tensor(o_masked[:, half], bank[bk][:, 0:H * NVC].rearrange("p (h d) -> p h d", h=H),
                                  e_sb[:, par, half].rearrange("p t h -> p (t h)").unsqueeze(2).to_broadcast([P, H, NVC]),
                                  ALU.mult).then_inc(masked_ready, 1)

            def normalise_o(b, half, bk):
                c = 2 * b + half
                dve.wait_ge(o_mm, c + 1)
                dve.wait_ge(masked_ready, c + 1)
                dve.tensor_tensor(o_sum[:, half], bank[bk][:].rearrange("p (h d) -> p h d", h=H)[:, :, 0:NVC],
                                  o_masked[:, half], ALU.add).then_inc(norm_step, 1)
                dve.wait_ge(norm_step, 3 * c + 1)
                dve.reciprocal(o_den[:, half, :], o_sum[:, half, :, HD]).then_inc(norm_step, 1)
                dve.wait_ge(norm_step, 3 * c + 2)
                wait(dve, oT_mm, c - 1)
                dve.tensor_tensor(o_tok[:, half].rearrange("p t (h d) -> p (t h) d", d=HD), o_sum[:, half, :, 0:HD],
                                  o_den[:, half].unsqueeze(2).to_broadcast([P, H, HD]),
                                  ALU.mult).then_inc(norm_step, 1)

            def run(st):
                n, p = st.n, st.par
                if st.has(0):
                    negate_and_split(n, 1)
                if st.has(2) and st.like > FIRST:
                    normalise(n + 2, p)
                if st.has(1):
                    maxima(n + 1, 0)
                    maxima(n + 1, 1)
                if st.has(2):
                    rest1(n + 2, p, "q", "B")
                if st.has(1):
                    maxima(n + 1, 2)
                if st.has(2):
                    rest1(n + 2, p, "k", "A")
                if st.has(-1):
                    masked_part(n - 1, 1 - p, 1, "B")
                if st.has(1):
                    negate_and_split(n + 1, 0)
                    maxima(n + 1, 3)
                if st.has(-1):
                    normalise_o(n - 1, 1, "A")
                if st.has(1):
                    b = n + 1
                    dve.wait_ge(v_mm, b + 1)
                    wait(dve, pv_mm, SLOTS * (b - 1))
                    wait(dve, suffix_mm, 2 * b - 2)
                    dve.tensor_tensor(v_sb[:, 1 - p, :, :, 0:HD], bank["B"][:].rearrange("p (t h d) -> p t h d", t=TB, h=H),
                                      bv_all[:].rearrange("p (h d) -> p h d", h=H).unsqueeze(1).to_broadcast([P, TB, H, HD]),
                                      ALU.add).then_inc(v_ready, 1)
                if st.has(0):
                    dve.wait_ge(ffn_mm, n + 1)
                    dve.wait_ge(xb_ready, n + 1)
                    dve.scalar_tensor_tensor(out=y1[:, p], in0=bank["A"][:].rearrange("p (t d) -> p t d", t=TB),
                                             scalar=ffn_scale[:, 0:1], in1=xb[:], op0=ALU.mult, op1=ALU.add).then_inc(y1_ready, 1)
                if st.has(1):
                    maxima(n + 1, 4)
                if st.has(2):
                    b = n + 2
                    dve.wait_ge(xT_ready, b + 1)
                    dve.tensor_scalar(x_over[:], xT[:, p], inv_in_scale[:, 0:1], FP8_MAX,
                                      ALU.mult, ALU.min).then_inc(quant_dve, 1)
                    dve.wait_ge(quant_dve, 4 * b + 1)
                    wait(dve, quant_pool, 2 * b)
                    dve.tensor_scalar(x_clip[:], x_over[:], -FP8_MAX, None, ALU.max).then_inc(quant_dve, 1)
                    dve.wait_ge(quant_dve, 4 * b + 2)
                    dve.tensor_scalar(x_exp[:].bitcast(I32), x_clip[:].bitcast(I32), 0x7F800000, None,
                                      ALU.bitwise_and).then_inc(quant_dve, 1)
                    dve.wait_ge(quant_dve, 4 * b + 3)
                    dve.tensor_scalar(x_big[:], x_exp[:], 2.0 ** -6, 1.5 * 2.0 ** 20, ALU.max, ALU.mult).then_inc(quant_dve, 1)
                if st.has(0):
                    masked_part(n, p, 0, "B")
                if st.has(1):
                    maxima(n + 1, 5)
                if st.has(-1):
                    b = n - 1
                    dve.wait_ge(proj_mm, b + 1)
                    wait(dve, out_landed[1 - p], 8 * (b - (1 - p)) + 16)
                    dve.tensor_tensor(y[:, 1 - p], bank["A"][:].rearrange("p (t d) -> p t d", t=TB), y1[:, 1 - p],
                                      ALU.add).then_inc(y_ready, 1)
                if st.has(0):
                    normalise_o(n, 0, "B")

            statistics(0)
            normalise(0, 0)
            dve.memset(v_sb[:, 0], 1.0)
            link(dve.memset(v_sb[:, 1], 1.0))
            fp8_weight()
            dve.wait_ge(w8_mm, 1)
            dve.tensor_copy(bqk_col[:], bank["A"][:, 0:2 * KT]).then_inc(w8T_ready, 1)
            dve.tensor_copy(w8T[:], ps2[:].bitcast(BF16)[:, 0:KT * D].rearrange("p (k o) -> p k o", k=KT)).then_inc(w8T_ready, 1)
            statistics(1)
            all_steps(dve, run)

        @block.tensor
        def _(pe):
            def take(st, bk, name):
                before = st.use_before(bk, name)
                if before:
                    who, b = before
                    s, per_batch, count = read[who]
                    pe.wait_ge(s, per_batch * b + count)
                return bank[bk]

            def phase1(b, par, i):
                half, j = i // 3, i % 3
                c = SLOTS * b + i
                wait(pe, max_done, c)
                if j == 0:
                    pe.wait_ge(stack_landed[half], 16 * STACK_DMAS * (b + 1))
                    for h in range(HALF):
                        hh = HALF * half + h
                        mm = pe.matmul(ps1[:, h * P:h * P + P], q_stack[0:K_MAX, par, hh, 0:P],
                                       k_stack[0:K_MAX, par, hh, 0:P], start=True, stop=True)
                else:
                    for h in range(4):
                        hh = HALF * half + 4 * (j - 1) + h
                        pe.matmul(ps1[:, h * S:h * S + P], q_stack[0:PROD, par, hh, P:S],
                                  k_stack[0:PROD, par, hh, 0:P], start=True, stop=True)
                        mm = pe.matmul(ps1[:, h * S + P:h * S + S], q_stack[0:K_MAX, par, hh, P:S],
                                       k_stack[0:K_MAX, par, hh, P:S], start=True, stop=True)
                mm.then_inc(ph1_mm, 1)

            def phase2(b, par, i):
                half, j = i // 3, i % 3
                wait(pe, exp_done, SLOTS * b + i)
                if j == 0:
                    pe.wait_ge(max_landed[half], 16 * PARTS * (b + 1))
                if j < 2:
                    for h in range(4):
                        hh = HALF * half + 4 * j + h
                        mm = pe.matmul(ps2[:, h * S:h * S + S], k_stack[0:K_SOFT, par, hh, 0:P],
                                       q_stack[0:K_SOFT, par, hh, :], start=True, stop=True)
                else:
                    for h in range(HALF):
                        hh = HALF * half + h
                        mm = pe.matmul(ps2[:, h * P:h * P + P], k_stack[0:K_SOFT, par, hh, P:S],
                                       q_stack[0:K_SOFT, par, hh, P:S], start=True, stop=True)
                mm.then_inc(ph2_mm, 1)

            def values(b, par, i):
                half, j = i // 3, i % 3
                pe.wait_ge(causal_done, SLOTS * b + i + 1)
                if j == 0:
                    wait(pe, o_raw_ready, 2 * (b - 1) + half + 1)
                    if half == 0:
                        pe.wait_ge(v_ready, b + 1)
                pr = probs[:, i % 2, :]
                if j < 2:
                    for q in range(4):
                        mm = pe.matmul(pso[32 * q:32 * q + 32, half, j, :], v_sb[:, par, 0, HALF * half + 4 * j + q, :],
                                       pr[:, q * S:q * S + S], start=(j == 0), stop=False, skip_group_check=True)
                else:
                    for g in range(2):
                        for q in range(4):
                            h = 4 * g + q
                            mm = pe.matmul(pso[32 * q:32 * q + 32, half, g, P:S], v_sb[:, par, 1, HALF * half + h, :],
                                           pr[:, h * P:h * P + P], start=False, stop=True, skip_group_check=True)
                mm.then_inc(pv_mm, 1)

            def transpose_x(st, b, par):
                pe.wait_ge(xn_ready, b + 1)
                dst = take(st, "B", "xT")
                for k in range(KT):
                    for t in range(TB):
                        mm = pe.transpose(dst[:, k * S + t * P:k * S + t * P + P], xn[:, par, t, k * P:k * P + P], ident[:])
                mm.then_inc(xT_mm, 1)

            def project_qk(st, b, par, qk, bk):
                j = "qk".index(qk)
                pe.wait_ge(xT_ready, b + 1)
                dst = take(st, bk, qk)
                for m in range(KT):
                    for k in range(KT):
                        col = j * D + m * P
                        mm = pe.matmul(dst[:, m * S:m * S + S], wqk_sb[:, k, col:col + P], xT[:, par, k, :],
                                       start=(k == 0), stop=(k == KT - 1))
                mm.then_inc((q_mm, k_mm)[j], 1)

            def tokens_by(dst, lhsT, rhs):
                for t in range(TB):
                    for k in range(KT):
                        mm = pe.matmul(dst[:, t * D:t * D + D], lhsT[:, k, t * P:t * P + P], rhs[:, k, :],
                                       start=(k == 0), stop=(k == KT - 1))
                return mm

            def transpose_max(st, b, half, bk):
                pe.wait_ge(neg_step, 6 * (2 * b + half) + 6)
                dst = take(st, bk, f"max_h{half}").ap().bitcast(BF16)
                for t in range(TB):
                    mm = pe.transpose(dst[0:PARTS * HALF, t * P:t * P + P],
                                      neg_parts[:, half, t].rearrange("p r h -> p (r h)"), ident_bf[:])
                mm.then_inc(max_mm, 1)

            def suffix(st, b, par, half):
                pe.wait_ge(v_ready, b + 1)
                dst = take(st, "B", f"suffix{half}")
                heads = slice(HALF * half, HALF * half + HALF)
                w = HALF * NVC
                pe.matmul(dst[:, 0:w], later[:], v_sb[:, par, 0, heads, 0:NVC], start=True, stop=False)
                pe.matmul(dst[:, 0:w], ones[:], v_sb[:, par, 1, heads, 0:NVC], start=False, stop=True)
                pe.matmul(dst[:, w:2 * w], later[:], v_sb[:, par, 1, heads, 0:NVC], start=True, stop=True).then_inc(suffix_mm, 1)

            def transpose_o(st, b, half, bk):
                pe.wait_ge(o_raw_ready, 2 * b + half + 1)
                dst = take(st, bk, f"o{half}")
                for t in range(TB):
                    for g in range(2):
                        at = (2 * t + g) * P
                        mm = pe.transpose(dst[:, at:at + P], o_raw[:, half, g, t * P:t * P + P], ident[:])
                mm.then_inc(o_mm, 1)

            def transpose_norm_o(st, b, half):
                pe.wait_ge(norm_step, 3 * (2 * b + half) + 3)
                dst = take(st, "A", f"norm_o{half}")
                for t in range(TB):
                    mm = pe.transpose(dst[:, t * P:t * P + P], o_tok[:, half, t, :], ident[:])
                mm.then_inc(oT_mm, 1)

            pe.wait_ge(const_ready, CONSTS)
            pe.wait_ge(scales_ready, 1)
            for k in range(KT):
                for o in range(KT):
                    mm = pe.transpose(ps2[:].bitcast(BF16)[:, k * D + o * P:k * D + o * P + P], w8_bf[:, o, k * P:k * P + P], ident_bf[:])
            pe.transpose(bank["A"][:, 0:2 * KT], bqk_ordered[:], ident[0:2 * KT, 0:2 * KT]).then_inc(w8_mm, 1)
            pe.wait_ge(w8T_ready, 2)
            pe.wait_ge(w_landed, 16)
            pe.wait_ge(w_ordered, 1)
            pe.wait_ge(wo_landed, 16)

            def run(st):
                n, p = st.n, st.par
                for i in range(SLOTS):
                    if st.has(1):
                        if st.like == -1 and i == 0:
                            pe.wait_ge(mask_landed, 8 * 16)
                            pe.wait_ge(ones_ready, 1)
                        phase1(n + 1, 1 - p, i)
                    if st.has(0):
                        phase2(n, p, i)
                    if i > 0 and st.has(0):
                        values(n, p, i - 1)
                    if i == 0 and st.has(-1):
                        values(n - 1, 1 - p, SLOTS - 1)
                    if i == 0:
                        if st.has(-1):
                            transpose_norm_o(st, n - 1, 0)
                        if st.has(2):
                            transpose_x(st, n + 2, p)
                    elif i == 1:
                        if st.has(0):
                            transpose_max(st, n, 1, "A")
                        if st.has(2):
                            project_qk(st, n + 2, p, "q", "B")
                    elif i == 2:
                        if st.has(2):
                            project_qk(st, n + 2, p, "k", "A")
                        if st.has(-1):
                            suffix(st, n - 1, 1 - p, 1)
                    elif i == 3:
                        if st.has(-1):
                            transpose_o(st, n - 1, 1, "A")
                        if st.has(1):
                            pe.wait_ge(xT_ready, n + 2)
                            tokens_by(take(st, "B", "v"), xT[:, 1 - p], wqkv_sb[:, :, 2 * D:]).then_inc(v_mm, 1)
                        if st.has(0):
                            pe.wait_ge(quant_pool, 2 * n + 2)
                            tokens_by(take(st, "A", "ffn"), xq[:, p], w8T[:]).then_inc(ffn_mm, 1)
                    elif i == 4:
                        if st.has(0):
                            suffix(st, n, p, 0)
                        if st.has(-1):
                            transpose_norm_o(st, n - 1, 1)
                        if st.has(1):
                            transpose_max(st, n + 1, 0, "B")
                    else:
                        if st.has(-1):
                            pe.wait_ge(oT_ready, 2 * n)
                            tokens_by(take(st, "A", "proj"), oT[:], wo_sb[:]).then_inc(proj_mm, 1)
                        if st.has(0):
                            transpose_o(st, n, 0, "B")

            all_steps(pe, run)


_INS = ["L0_attn_x", "L0_attn_Wqkv", "L0_attn_bqkv", "L0_attn_Wo", "L0_attn_bo", "L0_ffn_weight",
        "L0_ffn_weight_scale", "L0_ffn_input_scale"]


def kernel(**inputs):
    import numpy as _np
    import concourse.bacc as _bacc
    from concourse import mybir as _mybir
    from concourse.bass_utils import run_bass_kernel_spmd as _run

    nc = _bacc.Bacc("TRN2", target_bir_lowering=False, num_devices=1)
    arrays, args = {}, []
    for name in _INS:
        a = _np.ascontiguousarray(inputs[name])
        arrays[f"in_{name}_dram"] = a
        args.append(nc.dram_tensor(f"in_{name}_dram", a.shape, _mybir.dt.from_np(a.dtype), kind="ExternalInput").ap())
    args.append(nc.dram_tensor("out_0_dram", (B, S, D), _mybir.dt.float32, kind="ExternalOutput").ap())
    build(nc, *args)
    r = _run(nc, [arrays], core_ids=[0])
    return r.results[0]["out_0_dram"]
```

```python
from contextlib import ExitStack

import concourse.bass as bass
from concourse import mybir

ALU = mybir.AluOpType
ACT = mybir.ActivationFunctionType
AX_X = mybir.AxisListType.X
BF16 = mybir.dt.bfloat16
FP16 = mybir.dt.float16
F32 = mybir.dt.float32
I32 = mybir.dt.int32
U8 = mybir.dt.uint8
U16 = mybir.dt.uint16

P = 128
B = 8
S = 256
D = 256
H = 16
HD = D // H
TB = S // P
KT = D // P
HALF = H // 2
SLOTS = 6
EPS = 1e-5
SCALE = HD ** -0.5
MASKED = -10000.0 / SCALE
FP8_MAX = 448.0

PARTS = 3
Q_ORDER = (0, 1, 2, 0, 1, 0)
K_ORDER = (0, 0, 0, 1, 1, 2)
PROD = len(Q_ORDER) * HD
Q_READ = 112
ROW_MAX = PROD
ROW_MASK = PROD + PARTS
MB = 5
MASK_ROWS = -(-P // MB)
K_SOFT = PROD + PARTS
K_MAX = ROW_MASK + MASK_ROWS
G = 2.0 ** 24
MASK_C = 16.0
NVC = HD + 1

USES = {
    "A": [("norm_o0", -1), ("max_h1", 0), ("k", 2), ("o1", -1), ("ffn", 0), ("norm_o1", -1), ("proj", -1)],
    "B": [("xT", 2), ("q", 2), ("suffix1", -1), ("v", 1), ("suffix0", 0), ("max_h0", 1), ("o0", 0)],
}
USES_BEFORE = {"A": [("k", 0), ("k", 1)], "B": [("xT", 0), ("q", 0), ("xT", 1), ("q", 1)]}
FIRST, LAST = -1, B
LOOP = range(2, 6)


class Step:

    def __init__(self, n, like):
        self.n, self.like, self.par = n, like, like % 2

    def has(self, off):
        return 0 <= self.like + off < B and (off < 2 or self.like + off >= 2)

    def use_before(self, bank, name):
        if (name, self.like + 2) in USES_BEFORE[bank]:
            at = USES_BEFORE[bank].index((name, self.like + 2))
            return USES_BEFORE[bank][at - 1] if at else None
        order = [who for who, _ in USES[bank]]
        at, like, n = order.index(name), self.like, self.n
        while like >= FIRST:
            for who, off in reversed(USES[bank][:at]):
                if Step(n, like).has(off):
                    return who, n + off
            at, like, n = len(order), like - 1, n - 1
        return USES_BEFORE[bank][-1]


def all_steps(eng, run):
    for n in range(FIRST, LOOP.start):
        run(Step(n, n))
    with eng.Fori(0, len(LOOP) // 2) as turn:
        n = turn * 2 + LOOP.start
        run(Step(n, LOOP.start))
        run(Step(n + 1, LOOP.start + 1))
    for n in range(LOOP.stop, LAST + 1):
        run(Step(n, n))


def wait(eng, sem, value, passed=None):
    if not isinstance(value, int) or value > 0:
        eng.wait_ge(sem, value)
        if not isinstance(value, int) and passed is not None:
            eng.sem_inc(passed, 1)


def build(nc, x, wqkv, bqkv, wo, bo, w8, w8_scale, in_scale, out):
    ctx = ExitStack()
    with ctx:
        def sb(name, shape, dt=F32):
            return ctx.enter_context(nc.sbuf_tensor(name, shape, dt))

        def psum(name, shape, dt=F32):
            return ctx.enter_context(nc.psum_tensor(name, shape, dt))

        def sem(name):
            return ctx.enter_context(nc.semaphore(name))

        ident = sb("ident", [P, P])
        ident_bf = sb("ident_bf", [P, P], BF16)
        later = sb("later", [P, P])
        ones = sb("ones", [P, P])
        fixed_q = sb("fixed_q", [PARTS + MASK_ROWS, TB, P], BF16)
        fixed_k = sb("fixed_k", [PARTS + MASK_ROWS, TB, P], BF16)
        neg_floor = sb("neg_floor", [P, TB, HALF])
        wqkv_sb = sb("wqkv_sb", [P, KT, 3 * D])
        wqk_sb = sb("wqk_sb", [P, KT, 2 * D])
        wo_sb = sb("wo_sb", [P, KT, D])
        bqk_row = sb("bqk_row", [2 * KT, P])
        bqk_ordered = sb("bqk_ordered", [2 * KT, P])
        bqk_col = sb("bqk_col", [P, 2 * KT])
        bv_all = sb("bv_all", [P, D])
        bo_all = sb("bo_all", [P, D])
        w8_raw = sb("w8_raw", [P, KT, D], U8)
        w8_wide = sb("w8_wide", [P, KT, D], U16)
        w8_mag = sb("w8_mag", [P, KT, D], U16)
        w8_sign = sb("w8_sign", [P, KT, D], U16)
        w8_bits = sb("w8_bits", [P, KT, D], U16)
        w8_bf = sb("w8_bf", [P, KT, D], BF16)
        w8T = sb("w8T", [P, KT, D], BF16)
        in_scale_bf = sb("in_scale_bf", [P, 1], BF16)
        in_scale_f = sb("in_scale_f", [P, 1])
        w8_scale_f = sb("w8_scale_f", [P, 1])
        inv_in_scale = sb("inv_in_scale", [P, 1])
        ffn_scale = sb("ffn_scale", [P, 1])

        NT = B * TB
        x_all = sb("x_all", [P, NT, D])
        stats = sb("stats", [P, NT, 6])
        mean_var = sb("mean_var", [P, NT, 2])
        var_eps = sb("var_eps", [P, NT])
        std = sb("std", [P, NT])
        rstd0 = sb("rstd0", [P, NT])
        rstd_sq = sb("rstd_sq", [P, NT])
        rstd_e = sb("rstd_e", [P, NT])
        rstd_f = sb("rstd_f", [P, NT])
        rstd = sb("rstd", [P, NT])
        xn = sb("xn", [P, 2, TB, D])

        xT = sb("xT", [P, 2, KT, S])
        x_over = sb("x_over", [P, KT, S])
        x_clip = sb("x_clip", [P, KT, S])
        x_exp = sb("x_exp", [P, KT, S])
        x_big = sb("x_big", [P, KT, S])
        x_sum = sb("x_sum", [P, KT, S])
        xq = sb("xq", [P, 2, KT, S], BF16)
        parts = {qk: sb(f"{qk}_parts", [P, 2, PARTS, KT, S], BF16) for qk in "qk"}
        rest = {qk: sb(f"{qk}_rest", [P, KT, S]) for qk in "qk"}
        q_stack = sb("q_stack", [P, 2, H, S], BF16)
        k_stack = sb("k_stack", [P, 2, H, S], BF16)
        v_sb = sb("v_sb", [P, 2, TB, H, 32])
        row_max = sb("row_max", [P, 2, TB, HALF])
        neg_max = sb("neg_max", [P, 2, TB, HALF])
        neg_r1 = sb("neg_r1", [P, 2, TB, HALF])
        neg_parts = sb("neg_parts", [P, 2, TB, PARTS, HALF], BF16)
        e_arg = sb("e_arg", [P, 2, TB, HALF])
        e_sb = sb("e_sb", [P, 2, 2, TB, HALF])
        max_rows = sb("max_rows", [PARTS * HALF, 2, S], BF16)
        probs = sb("probs", [P, 2, 1024])
        o_raw = sb("o_raw", [P, 2, 2, S])
        o_masked = sb("o_masked", [P, 2, H, NVC])
        o_sum = sb("o_sum", [P, 2, H, NVC])
        o_den = sb("o_den", [P, 2, H])
        o_tok = sb("o_tok", [P, 2, TB, P])
        oT = sb("oT", [P, KT, S])
        xb = sb("xb", [P, TB, D])
        y1 = sb("y1", [P, 2, TB, D])
        y = sb("y", [P, 2, TB, D])

        scratch = {qk: nc.dram_tensor(f"{qk}_scratch", (2, rows, HALF, 2, S), BF16, kind="Internal").ap()
                   for qk, rows in (("q", Q_READ), ("k", PROD))}
        ps1 = psum("ps1", [P, 1024])
        ps2 = psum("ps2", [P, 1024])
        pso = psum("pso", [P, 2, 2, S])
        bank = {"A": psum("bankA", [P, 512]), "B": psum("bankB", [P, 512])}

        x_landed = [sem(f"x{g}_landed") for g in range(3)]
        w_landed, bqk_landed, ffn_landed = sem("w_landed"), sem("bqk_landed"), sem("ffn_landed")
        wv_landed, proj_landed = sem("wv_landed"), sem("proj_landed")
        passed = sem("passed")
        floor_ready = sem("floor_ready")
        const_ready, pool_chain = sem("const_ready"), sem("pool_chain")
        w_ordered = sem("w_ordered")
        mask_landed = sem("mask_landed")
        init_dve = sem("init_dve")
        bqk_ready, bqk_mm, bqk_col_ready = sem("bqk_ready"), sem("bqk_mm"), sem("bqk_col_ready")
        v_ones_ready = sem("v_ones_ready")
        std_ready = sem("std_ready")
        dve_chain, w8_mm, w8T_ready = sem("dve_chain"), sem("w8_mm"), sem("w8T_ready")
        w8_ready = sem("w8_ready")
        xn_ready, xT_mm, xT_ready = sem("xn_ready"), sem("xT_mm"), sem("xT_ready")
        q_mm, k_mm, v_mm = sem("q_mm"), sem("k_mm"), sem("v_mm")
        part1_ready, rest_ready = sem("part1_ready"), sem("rest_ready")
        part2_ready, split_ready = sem("part2_ready"), sem("split_ready")
        spilled = [sem(f"{qk}_spilled") for qk in "qk"]
        stack_landed = [sem(f"stack_landed{h}") for h in range(2)]
        v_ready = sem("v_ready")
        ph1_mm, max_done = sem("ph1_mm"), sem("max_done")
        neg_step, max_mm, max_rows_ready = sem("neg_step"), sem("max_mm"), sem("max_rows_ready")
        max_landed = [sem(f"max_landed{h}") for h in range(2)]
        e_ready = sem("e_ready")
        ph2_mm, exp_done, causal_done, pv_mm = sem("ph2_mm"), sem("exp_done"), sem("causal_done"), sem("pv_mm")
        o_raw_ready, o_mm, suffix_mm = sem("o_raw_ready"), sem("o_mm"), sem("suffix_mm")
        masked_ready, norm_step = sem("masked_ready"), sem("norm_step")
        oT_mm, oT_ready = sem("oT_mm"), sem("oT_ready")
        quant_dve, quant_pool = sem("quant_dve"), sem("quant_pool")
        ffn_mm, xb_ready, y1_ready = sem("ffn_mm"), sem("xb_ready"), sem("y1_ready")
        proj_mm, y_ready = sem("proj_mm"), sem("y_ready")
        out_landed = [sem(f"out_landed{p}") for p in range(2)]
        read = {"xT": (xT_ready, 1, 1), "q": (rest_ready, 2, 1), "k": (rest_ready, 2, 2),
                "v": (v_ready, 1, 1), "max_h0": (max_rows_ready, 2, 1), "max_h1": (max_rows_ready, 2, 2),
                "suffix0": (masked_ready, 2, 1), "suffix1": (masked_ready, 2, 2),
                "o0": (norm_step, 6, 1), "o1": (norm_step, 6, 4),
                "norm_o0": (oT_ready, 2, 1), "norm_o1": (oT_ready, 2, 2),
                "ffn": (y1_ready, 1, 1), "proj": (y_ready, 1, 1)}

        STACK_DMAS = 2
        SPILL_DMAS = 3
        MASK_DMAS = 6
        CONSTS = 3
        X_GROUPS = ((0, TB), (TB, 2 * TB), (2 * TB, B * TB))

        x_tok = x.rearrange("b (t p) d -> p (b t) d", p=P)
        block = ctx.enter_context(nc.Block())

        @block.sync
        def _(sp):
            for par in range(2):
                sp.sem_inc(out_landed[par], 16)
            def load_x(g):
                lo, hi = X_GROUPS[g]
                sp.dma_start(x_all[:, lo:hi, :], x_tok[:, lo:hi, :]).then_inc(x_landed[g], 16)

            w_in = wqkv.rearrange("(k p) n -> p k n", p=P)
            load_x(0)
            sp.dma_start(wqkv_sb[:, :, 0:2 * D], w_in[:, :, 0:2 * D]).then_inc(w_landed, 16)
            sp.dma_start(bqk_row[:], bqkv[0:2 * D].rearrange("(m p) -> m p", p=P)).then_inc(bqk_landed, 16)
            load_x(1)
            for t, src in ((in_scale_bf[:], in_scale.partition_broadcast(P)),
                           (w8_scale_f[:], w8_scale.partition_broadcast(P)),
                           (w8_raw[:], w8.bitcast(U8).rearrange("(k p) n -> p k n", p=P))):
                sp.dma_start(t, src).then_inc(ffn_landed, 16)
            sp.dma_start(wqkv_sb[:, :, 2 * D:], w_in[:, :, 2 * D:]).then_inc(wv_landed, 16)
            sp.dma_start(bv_all[:], bqkv[2 * D:3 * D].partition_broadcast(P)).then_inc(wv_landed, 16)
            again = Q_READ - ROW_MAX
            sp.wait_ge(const_ready, CONSTS)
            for par in range(2):
                for dst, rows in ((scratch["q"][par, ROW_MAX:Q_READ].rearrange("r h k t -> r (h k) t"), fixed_q[0:again]),
                                  (k_stack[ROW_MAX:K_MAX, par], fixed_k[:]),
                                  (q_stack[Q_READ:K_MAX, par], fixed_q[again:])):
                    r = rows.shape[0]
                    sp.dma_start(dst, rows.rearrange("r t p -> r (t p)").unsqueeze(1).to_broadcast([r, H, S])).then_inc(mask_landed, 16)
            load_x(2)
            sp.dma_start(bo_all[:], bo.partition_broadcast(P)).then_inc(proj_landed, 16)
            sp.dma_start(wo_sb[:], wo.rearrange("(k p) n -> p k n", p=P)).then_inc(proj_landed, 16)
            sp.wait_ge(mask_landed, MASK_DMAS * 16)

            def spill(b, par, qk):
                j = "qk".index(qk)
                wait(sp, split_ready, 2 * b + j + 1, passed)
                for half in range(2):
                    wait(sp, stack_landed[half], 16 * STACK_DMAS * (b - 1), passed)
                row = 0
                for parts_of in ((0, 1, 2), (0, 1), (0,)) if qk == "q" else ((0, 0, 0), (1, 1), (2,)):
                    c = len(parts_of)
                    src = parts[qk][:, par, parts_of[0]:parts_of[-1] + 1].rearrange("p i k t -> p i (k t)")
                    if qk == "k":
                        src = src.to_broadcast([P, c, KT * S])
                    sp.dma_start(scratch[qk][par, row:row + HD * c].rearrange("(i d) h k t -> (d h) i (k t)", i=c),
                                 src).then_inc(spilled[j], 16)
                    row += HD * c

            def stack(b, par, half):
                wait(sp, ph2_mm, SLOTS * (b - 2) + 3 * half + 3, passed)
                heads = slice(HALF * half, HALF * half + HALF)
                for j, (stack_sb, qk, rows) in enumerate(((q_stack, "q", Q_READ), (k_stack, "k", PROD))):
                    wait(sp, spilled[j], 16 * SPILL_DMAS * (b + 1), passed)
                    sp.dma_start(stack_sb[0:rows, par, heads, :],
                                 scratch[qk][par, :, :, half, :]).then_inc(stack_landed[half], 16)

            def max_to_stack(b, par, half):
                wait(sp, max_rows_ready, 2 * b + half + 1, passed)
                for r in range(PARTS):
                    sp.dma_start(q_stack[ROW_MAX + r:ROW_MAX + r + 1, par, HALF * half:HALF * half + HALF, :],
                                 max_rows[HALF * r:HALF * r + HALF, half, :]).then_inc(max_landed[half], 16)

            def run(st):
                n, p = st.n, st.par
                if st.has(0):
                    max_to_stack(n, p, 1)
                if st.has(2):
                    spill(n + 2, p, "q")
                    spill(n + 2, p, "k")
                    stack(n + 2, p, 0)
                if st.has(1):
                    max_to_stack(n + 1, 1 - p, 0)
                if st.has(-1):
                    wait(sp, y_ready, n, passed)
                    sp.dma_start(out[bass.ds(n - 1, 1)].rearrange("b (t p) d -> p (b t) d", p=P),
                                 y[:, 1 - p]).then_inc(out_landed[1 - p], 16)
                if st.has(2):
                    stack(n + 2, p, 1)

            for b in range(2):
                spill(b, b, "q")
                spill(b, b, "k")
                stack(b, b, 0)
                stack(b, b, 1)
            all_steps(sp, run)
            for par in range(2):
                sp.wait_ge(out_landed[par], 16 + 16 * B // 2)

        @block.gpsimd
        def _(pool):
            steps = [0]

            def link(ins):
                steps[0] += 1
                ins.then_inc(pool_chain, 1)
                pool.wait_ge(pool_chain, steps[0])

            pool.memset(ident[:], 0.0)
            pool.memset(later[:], 1.0)
            pool.memset(ones[:], 1.0)
            pool.memset(fixed_q[:], 0.0)
            link(pool.memset(fixed_k[:], 0.0))
            link(pool.affine_select(out=ident[:], in_=ident[:], compare_op=ALU.not_equal, fill=1.0,
                                    base=0, pattern=[[-1, P]], channel_multiplier=1))
            pool.tensor_copy(ident_bf[:], ident[:]).then_inc(const_ready, 1)
            link(pool.memset(fixed_k[0:PARTS], 1.0))
            link(pool.affine_select(out=fixed_q[:], in_=fixed_q[:], compare_op=ALU.is_ge, fill=G,
                                    base=MB * PARTS, pattern=[[0, TB], [1, P]], channel_multiplier=-MB))
            for j in range(MB):
                link(pool.affine_select(out=fixed_q[:], in_=fixed_q[:], compare_op=ALU.not_equal, fill=G ** -j,
                                        base=MB * PARTS - j, pattern=[[0, TB], [1, P]], channel_multiplier=-MB))
                ins = pool.affine_select(out=fixed_k[:], in_=fixed_k[:], compare_op=ALU.not_equal,
                                         fill=-MASK_C * G ** j,
                                         base=MB * PARTS - j, pattern=[[0, TB], [1, P]], channel_multiplier=-MB)
                if j < MB - 1:
                    link(ins)
            ins.then_inc(const_ready, 1)
            pool.affine_select(out=later[:], in_=later[:], compare_op=ALU.is_gt, fill=0.0,
                               base=0, pattern=[[-1, P]], channel_multiplier=1).then_inc(const_ready, 1)
            link(pool.memset(neg_floor[:], -MASKED))
            pool.affine_select(out=neg_floor[:, TB - 1], in_=neg_floor[:, TB - 1], compare_op=ALU.not_equal,
                               fill=3.0e38, base=-(P - 1), pattern=[[0, HALF]],
                               channel_multiplier=1).then_inc(floor_ready, 1)
            pool.wait_ge(floor_ready, 1)

            def causal(b, i):
                c = SLOTS * b + i
                wait(pool, exp_done, c + 1, passed)
                pr = probs[:, i % 2, :]
                if i % 3 < 2:
                    v, heads = pr.rearrange("p (h t) -> p h t", h=4)[:, :, 0:P], 4
                else:
                    v, heads = pr.rearrange("p (h t) -> p h t", h=HALF), HALF
                pool.affine_select(out=v, in_=v, compare_op=ALU.is_ge, fill=0.0, base=0,
                                   pattern=[[0, heads], [1, P]], channel_multiplier=-1).then_inc(causal_done, 1)

            def split(b, par, qk):
                j = "qk".index(qk)
                pt, r = parts[qk], rest[qk]
                wait(pool, rest_ready, 2 * b + j + 1, passed)
                pool.tensor_scalar(pt[:, par, 1], r[:], 1.0, 1.0, ALU.mult, ALU.mult).then_inc(part2_ready, 1)
                wait(pool, part2_ready, 2 * b + j + 1, passed)
                pool.tensor_tensor(pt[:, par, 2], r[:], pt[:, par, 1], ALU.subtract).then_inc(split_ready, 1)

            def round_x(b, par):
                wait(pool, quant_dve, 4 * b + 4, passed)
                pool.tensor_tensor(x_sum[:], x_clip[:], x_big[:], ALU.add).then_inc(quant_pool, 1)
                wait(pool, quant_pool, 2 * b + 1, passed)
                wait(pool, ffn_mm, b - 1, passed)
                pool.tensor_tensor(xq[:, par], x_sum[:], x_big[:], ALU.subtract).then_inc(quant_pool, 1)

            def run(st):
                n, p = st.n, st.par
                if st.has(0):
                    causal(n, 0)
                    causal(n, 1)
                    causal(n, 2)
                if st.has(2):
                    split(n + 2, p, "q")
                if st.has(0):
                    wait(pool, y1_ready, n, passed)
                    if st.like == 0:
                        pool.wait_ge(proj_landed, 2 * 16)
                        for g in range(3):
                            pool.wait_ge(x_landed[g], 16)
                    pool.tensor_tensor(xb[:], x_all[:, bass.ds(TB * n, TB), :],
                                       bo_all[:].unsqueeze(1).to_broadcast([P, TB, D]),
                                       ALU.add).then_inc(xb_ready, 1)
                if st.has(2):
                    split(n + 2, p, "k")
                if st.has(0):
                    causal(n, 3)
                if st.has(0):
                    causal(n, 4)
                if st.has(2):
                    round_x(n + 2, p)
                if st.has(0):
                    causal(n, 5)

            for b in range(2):
                split(b, b, "q")
                split(b, b, "k")
            for b in range(2):
                round_x(b, b)
            all_steps(pool, run)

        @block.scalar
        def _(act):
            def square_roots(g):
                lo, hi = X_GROUPS[g]
                act.wait_ge(init_dve, 2 * g + 1)
                act.activation(std[:, lo:hi], var_eps[:, lo:hi], ACT.Sqrt).then_inc(std_ready, 1)

            def exponentials(b, i):
                c = SLOTS * b + i
                act.wait_ge(ph2_mm, c + 1)
                wait(act, pv_mm, c - 1)
                act.activation(probs[:, i % 2, :], ps2[:], ACT.Exp, scale=SCALE).then_inc(exp_done, 1)

            def part1(b, par, qk, bk):
                j = "qk".index(qk)
                act.wait_ge((q_mm, k_mm)[j], b + 1)
                wait(act, spilled[j], 16 * SPILL_DMAS * (b - 1))
                for half in range(2):
                    ins = act.activation(parts[qk][:, par, 0, half, :], bank[bk][:, half * S:half * S + S],
                                         ACT.Identity, bias=bqk_col[:, KT * j + half:KT * j + half + 1])
                ins.then_inc(part1_ready, 1)

            def o_out(b, half):
                c = 2 * b + half
                act.wait_ge(pv_mm, SLOTS * b + 3 * half + 3)
                wait(act, o_mm, c - 1)
                act.activation(o_raw[:, half], pso[:, half], ACT.Copy).then_inc(o_raw_ready, 1)

            def oT_out(b, half, bk):
                c = 2 * b + half
                act.wait_ge(oT_mm, c + 1)
                wait(act, proj_mm, b)
                act.activation(oT[:, half], bank[bk][:, 0:S], ACT.Copy).then_inc(oT_ready, 1)

            def max_out(b, par, half, bk):
                c = 2 * b + half
                act.wait_ge(neg_step, SLOTS * c + 6)
                wait(act, masked_ready, c - 3)
                act.activation(e_sb[:, par, half], e_arg[:, half], ACT.Exp, scale=SCALE).then_inc(e_ready, 1)
                act.wait_ge(max_mm, c + 1)
                wait(act, max_landed[half], 16 * PARTS * b)
                act.activation(max_rows[:, half, :], bank[bk].ap().bitcast(BF16)[0:PARTS * HALF, 0:S],
                               ACT.Copy).then_inc(max_rows_ready, 1)

            def xT_out(b, par):
                act.wait_ge(xT_mm, b + 1)
                wait(act, v_mm, b - 1)
                wait(act, quant_dve, 4 * (b - 2) + 1)
                act.activation(xT[:, par], bank["B"][:].rearrange("p (k s) -> p k s", k=KT), ACT.Copy).then_inc(xT_ready, 1)

            def run(st):
                n, p = st.n, st.par
                if st.has(0):
                    exponentials(n, 0)
                if st.has(-1):
                    o_out(n - 1, 1)
                    oT_out(n - 1, 0, "A")
                if st.has(2):
                    xT_out(n + 2, p)
                if st.has(0):
                    exponentials(n, 1)
                    max_out(n, p, 1, "A")
                if st.has(2):
                    part1(n + 2, p, "q", "B")
                if st.has(0):
                    exponentials(n, 2)
                if st.has(2):
                    part1(n + 2, p, "k", "A")
                if st.has(0):
                    exponentials(n, 3)
                    o_out(n, 0)
                    exponentials(n, 4)
                if st.has(-1):
                    oT_out(n - 1, 1, "A")
                if st.has(1):
                    max_out(n + 1, 1 - p, 0, "B")
                if st.has(0):
                    exponentials(n, 5)

            square_roots(0)
            act.wait_ge(w_landed, 16)
            for k in range(KT):
                ins = act.activation(wqk_sb[:, k].rearrange("p (m d h) -> p m d h", m=2 * KT, d=HD),
                                     wqkv_sb[:, k, 0:2 * D].rearrange("p (m h d) -> p m d h", m=2 * KT, d=HD), ACT.Copy)
            ins.then_inc(w_ordered, 1)
            square_roots(1)
            for b in range(2):
                xT_out(b, b)
                if b == 0:
                    act.wait_ge(bqk_col_ready, 1)
                part1(b, b, "q", "B")
                part1(b, b, "k", "A")
            square_roots(2)
            all_steps(act, run)

        @block.vector
        def _(dve):
            steps = [0]

            def link(ins, s=dve_chain):
                steps[0] += 1
                ins.then_inc(s, 1)
                dve.wait_ge(s, steps[0])

            def statistics(g):
                lo, hi = X_GROUPS[g]
                dve.wait_ge(x_landed[g], 16)
                for t in range(lo, hi):
                    ins = dve.bn_stats(stats[:, t, :], x_all[:, t, :])
                link(ins)
                for t in range(lo, hi):
                    ins = dve.bn_aggr(mean_var[:, t, :], stats[:, t, :])
                link(ins)
                dve.tensor_scalar(var_eps[:, lo:hi], mean_var[:, lo:hi, 1], EPS, None, ALU.add).then_inc(init_dve, 1)
                dve.wait_ge(std_ready, g + 1)
                link(dve.reciprocal(rstd0[:, lo:hi], std[:, lo:hi]))
                link(dve.tensor_tensor(rstd_sq[:, lo:hi], rstd0[:, lo:hi], rstd0[:, lo:hi], ALU.mult))
                link(dve.tensor_tensor(rstd_e[:, lo:hi], rstd_sq[:, lo:hi], var_eps[:, lo:hi], ALU.mult))
                link(dve.tensor_scalar(rstd_f[:, lo:hi], rstd_e[:, lo:hi], -0.5, 1.5, ALU.mult, ALU.add))
                dve.tensor_tensor(rstd[:, lo:hi], rstd0[:, lo:hi], rstd_f[:, lo:hi], ALU.mult).then_inc(init_dve, 1)
                dve.wait_ge(init_dve, 2 * g + 2)

            def normalise(b, par):
                wait(dve, xT_mm, b - 1)
                for t in range(TB):
                    i = TB * b + t
                    ins = dve.tensor_scalar(xn[:, par, t, :], x_all[:, bass.ds(i, 1), :].rearrange("p t d -> p (t d)"),
                                            mean_var[:, bass.ds(i, 1), 0], rstd[:, bass.ds(i, 1)],
                                            ALU.subtract, ALU.mult)
                ins.then_inc(xn_ready, 1)

            def scales():
                dve.wait_ge(ffn_landed, 3 * 16)
                link(dve.tensor_copy(in_scale_f[:], in_scale_bf[:]))
                dve.tensor_tensor(ffn_scale[:], in_scale_f[:], w8_scale_f[:], ALU.mult)
                link(dve.reciprocal(inv_in_scale[:], in_scale_f[:]))

            def fp8_weight():
                link(dve.tensor_copy(w8_wide[:], w8_raw[:]))
                dve.tensor_scalar(w8_mag[:], w8_wide[:], 0x7F, 7, ALU.bitwise_and, ALU.logical_shift_left)
                link(dve.tensor_scalar(w8_sign[:], w8_wide[:], 0x80, 8, ALU.bitwise_and, ALU.logical_shift_left))
                link(dve.tensor_tensor(w8_bits[:], w8_mag[:], w8_sign[:], ALU.bitwise_or))
                dve.tensor_scalar(w8_bf[:], w8_bits[:].bitcast(FP16), 256.0, None, ALU.mult).then_inc(w8_ready, 1)

            def clip_x(b, par):
                dve.wait_ge(xT_ready, b + 1)
                dve.tensor_scalar(x_over[:], xT[:, par], inv_in_scale[:, 0:1], FP8_MAX,
                                  ALU.mult, ALU.min).then_inc(quant_dve, 1)
                dve.wait_ge(quant_dve, 4 * b + 1)
                wait(dve, quant_pool, 2 * b)
                dve.tensor_scalar(x_clip[:], x_over[:], -FP8_MAX, None, ALU.max).then_inc(quant_dve, 1)
                dve.wait_ge(quant_dve, 4 * b + 2)
                dve.tensor_scalar(x_exp[:].bitcast(I32), x_clip[:].bitcast(I32), 0x7F800000, None,
                                  ALU.bitwise_and).then_inc(quant_dve, 1)
                dve.wait_ge(quant_dve, 4 * b + 3)
                dve.tensor_scalar(x_big[:], x_exp[:], 2.0 ** -6, 1.5 * 2.0 ** 20, ALU.max, ALU.mult).then_inc(quant_dve, 1)

            def maxima(b, i):
                half, j = i // 3, i % 3
                dve.wait_ge(ph1_mm, SLOTS * b + i + 1)
                if j == 0:
                    src, dst = ps1[:].rearrange("p (h s) -> p h s", h=HALF), row_max[:, half, 0, :]
                else:
                    src, dst = ps1[:].rearrange("p (h s) -> p h s", h=4), row_max[:, half, 1, 4 * j - 4:4 * j]
                dve.tensor_reduce(dst, src, AX_X, ALU.max).then_inc(max_done, 1)

            def negate_and_split(b, half):
                c = 2 * b + half
                at = SLOTS * c
                dve.wait_ge(max_done, SLOTS * b + 3 * half + 3)
                wait(dve, e_ready, c - 1)
                dve.scalar_tensor_tensor(out=neg_max[:, half], in0=row_max[:, half], scalar=-1.0,
                                         in1=neg_floor[:], op0=ALU.mult, op1=ALU.min).then_inc(neg_step, 1)
                dve.wait_ge(neg_step, at + 1)
                wait(dve, max_mm, c - 1)
                dve.tensor_copy(neg_parts[:, half, :, 0, :], neg_max[:, half]).then_inc(neg_step, 1)
                dve.tensor_scalar(e_arg[:, half], neg_max[:, half], MASKED, 0.0, ALU.add, ALU.min).then_inc(neg_step, 1)
                dve.wait_ge(neg_step, at + 2)
                dve.tensor_tensor(neg_r1[:, half], neg_max[:, half], neg_parts[:, half, :, 0, :],
                                  ALU.subtract).then_inc(neg_step, 1)
                dve.wait_ge(neg_step, at + 4)
                dve.tensor_copy(neg_parts[:, half, :, 1, :], neg_r1[:, half]).then_inc(neg_step, 1)
                dve.wait_ge(neg_step, at + 5)
                dve.tensor_tensor(neg_parts[:, half, :, 2, :], neg_r1[:, half], neg_parts[:, half, :, 1, :],
                                  ALU.subtract).then_inc(neg_step, 1)

            def rest1(b, par, qk, bk):
                j = "qk".index(qk)
                dve.wait_ge(part1_ready, 2 * b + j + 1)
                wait(dve, split_ready, 2 * (b - 1) + j + 1)
                for half in range(2):
                    ins = dve.scalar_tensor_tensor(out=rest[qk][:, half, :], in0=bank[bk][:, half * S:half * S + S],
                                                   scalar=bqk_col[:, KT * j + half:KT * j + half + 1],
                                                   in1=parts[qk][:, par, 0, half, :], op0=ALU.add, op1=ALU.subtract)
                ins.then_inc(rest_ready, 1)

            def masked_part(b, par, half, bk):
                c = 2 * b + half
                dve.wait_ge(suffix_mm, c + 1)
                dve.wait_ge(e_ready, c + 1)
                wait(dve, norm_step, 3 * (c - 2) + 1)
                dve.tensor_tensor(o_masked[:, half], bank[bk][:, 0:H * NVC].rearrange("p (h d) -> p h d", h=H),
                                  e_sb[:, par, half].rearrange("p t h -> p (t h)").unsqueeze(2).to_broadcast([P, H, NVC]),
                                  ALU.mult).then_inc(masked_ready, 1)

            def normalise_o(b, half, bk):
                c = 2 * b + half
                dve.wait_ge(o_mm, c + 1)
                dve.wait_ge(masked_ready, c + 1)
                dve.tensor_tensor(o_sum[:, half], bank[bk][:].rearrange("p (h d) -> p h d", h=H)[:, :, 0:NVC],
                                  o_masked[:, half], ALU.add).then_inc(norm_step, 1)
                dve.wait_ge(norm_step, 3 * c + 1)
                dve.reciprocal(o_den[:, half, :], o_sum[:, half, :, HD]).then_inc(norm_step, 1)
                dve.wait_ge(norm_step, 3 * c + 2)
                wait(dve, oT_mm, c - 1)
                dve.tensor_tensor(o_tok[:, half].rearrange("p t (h d) -> p (t h) d", d=HD), o_sum[:, half, :, 0:HD],
                                  o_den[:, half].unsqueeze(2).to_broadcast([P, H, HD]),
                                  ALU.mult).then_inc(norm_step, 1)

            def run(st):
                n, p = st.n, st.par
                if st.has(2):
                    normalise(n + 2, p)
                if st.has(0):
                    negate_and_split(n, 1)
                if st.has(1):
                    maxima(n + 1, 0)
                    maxima(n + 1, 1)
                if st.has(2):
                    rest1(n + 2, p, "q", "B")
                if st.has(1):
                    maxima(n + 1, 2)
                if st.has(2):
                    rest1(n + 2, p, "k", "A")
                if st.has(-1):
                    masked_part(n - 1, 1 - p, 1, "B")
                if st.has(1):
                    negate_and_split(n + 1, 0)
                    maxima(n + 1, 3)
                if st.has(-1):
                    normalise_o(n - 1, 1, "A")
                if st.has(1):
                    b = n + 1
                    dve.wait_ge(v_mm, b + 1)
                    wait(dve, pv_mm, SLOTS * (b - 1))
                    wait(dve, suffix_mm, 2 * b - 2)
                    dve.tensor_tensor(v_sb[:, 1 - p, :, :, 0:HD], bank["B"][:].rearrange("p (t h d) -> p t h d", t=TB, h=H),
                                      bv_all[:].rearrange("p (h d) -> p h d", h=H).unsqueeze(1).to_broadcast([P, TB, H, HD]),
                                      ALU.add).then_inc(v_ready, 1)
                if st.has(0):
                    dve.wait_ge(ffn_mm, n + 1)
                    dve.wait_ge(xb_ready, n + 1)
                    dve.scalar_tensor_tensor(out=y1[:, p], in0=bank["A"][:].rearrange("p (t d) -> p t d", t=TB),
                                             scalar=ffn_scale[:, 0:1], in1=xb[:], op0=ALU.mult, op1=ALU.add).then_inc(y1_ready, 1)
                if st.has(1):
                    maxima(n + 1, 4)
                if st.has(0):
                    masked_part(n, p, 0, "B")
                if st.has(2):
                    clip_x(n + 2, p)
                if st.has(1):
                    maxima(n + 1, 5)
                if st.has(0):
                    normalise_o(n, 0, "B")
                if st.has(-1):
                    b = n - 1
                    dve.wait_ge(proj_mm, b + 1)
                    wait(dve, out_landed[1 - p], 8 * (b - (1 - p)) + 16)
                    dve.tensor_tensor(y[:, 1 - p], bank["A"][:].rearrange("p (t d) -> p t d", t=TB), y1[:, 1 - p],
                                      ALU.add).then_inc(y_ready, 1)

            statistics(0)
            normalise(0, 0)
            dve.wait_ge(bqk_landed, 16)
            dve.tensor_copy(bqk_ordered[:].rearrange("m (d h) -> m d h", d=HD),
                            bqk_row[:].rearrange("m (h d) -> m d h", d=HD)).then_inc(bqk_ready, 1)
            statistics(1)
            normalise(1, 1)
            dve.wait_ge(bqk_mm, 1)
            dve.tensor_copy(bqk_col[:], ps1[:, 0:2 * KT]).then_inc(bqk_col_ready, 1)
            scales()
            dve.memset(v_sb[:, 0], 1.0)
            dve.memset(v_sb[:, 1], 1.0).then_inc(v_ones_ready, 1)
            dve.wait_ge(bqk_col_ready, 1)
            dve.wait_ge(v_ones_ready, 1)
            for b in range(2):
                rest1(b, b, "q", "B")
                rest1(b, b, "k", "A")
            clip_x(0, 0)
            fp8_weight()
            clip_x(1, 1)
            statistics(2)
            dve.wait_ge(w8_mm, 1)
            dve.tensor_copy(w8T[:], ps2[:].bitcast(BF16)[:, 0:KT * D].rearrange("p (k o) -> p k o", k=KT)).then_inc(w8T_ready, 1)
            dve.wait_ge(floor_ready, 1)
            dve.wait_ge(wv_landed, 2 * 16)
            all_steps(dve, run)

        @block.tensor
        def _(pe):
            def take(st, bk, name):
                before = st.use_before(bk, name)
                if before:
                    who, b = before
                    s, per_batch, count = read[who]
                    pe.wait_ge(s, per_batch * b + count)
                return bank[bk]

            def phase1(b, par, i):
                half, j = i // 3, i % 3
                c = SLOTS * b + i
                wait(pe, max_done, c)
                if j == 0:
                    pe.wait_ge(stack_landed[half], 16 * STACK_DMAS * (b + 1))
                    for h in range(HALF):
                        hh = HALF * half + h
                        mm = pe.matmul(ps1[:, h * P:h * P + P], q_stack[0:K_MAX, par, hh, 0:P],
                                       k_stack[0:K_MAX, par, hh, 0:P], start=True, stop=True)
                else:
                    for h in range(4):
                        hh = HALF * half + 4 * (j - 1) + h
                        pe.matmul(ps1[:, h * S:h * S + P], q_stack[0:PROD, par, hh, P:S],
                                  k_stack[0:PROD, par, hh, 0:P], start=True, stop=True)
                        mm = pe.matmul(ps1[:, h * S + P:h * S + S], q_stack[0:K_MAX, par, hh, P:S],
                                       k_stack[0:K_MAX, par, hh, P:S], start=True, stop=True)
                mm.then_inc(ph1_mm, 1)

            def phase2(b, par, i):
                half, j = i // 3, i % 3
                wait(pe, exp_done, SLOTS * b + i)
                if j == 0:
                    pe.wait_ge(max_landed[half], 16 * PARTS * (b + 1))
                if j < 2:
                    for h in range(4):
                        hh = HALF * half + 4 * j + h
                        mm = pe.matmul(ps2[:, h * S:h * S + S], k_stack[0:K_SOFT, par, hh, 0:P],
                                       q_stack[0:K_SOFT, par, hh, :], start=True, stop=True)
                else:
                    for h in range(HALF):
                        hh = HALF * half + h
                        mm = pe.matmul(ps2[:, h * P:h * P + P], k_stack[0:K_SOFT, par, hh, P:S],
                                       q_stack[0:K_SOFT, par, hh, P:S], start=True, stop=True)
                mm.then_inc(ph2_mm, 1)

            def values(b, par, i):
                half, j = i // 3, i % 3
                pe.wait_ge(causal_done, SLOTS * b + i + 1)
                if j == 0:
                    wait(pe, o_raw_ready, 2 * (b - 1) + half + 1)
                    if half == 0:
                        pe.wait_ge(v_ready, b + 1)
                pr = probs[:, i % 2, :]
                if j < 2:
                    for q in range(4):
                        mm = pe.matmul(pso[32 * q:32 * q + 32, half, j, :], v_sb[:, par, 0, HALF * half + 4 * j + q, :],
                                       pr[:, q * S:q * S + S], start=(j == 0), stop=False, skip_group_check=True)
                else:
                    for g in range(2):
                        for q in range(4):
                            h = 4 * g + q
                            mm = pe.matmul(pso[32 * q:32 * q + 32, half, g, P:S], v_sb[:, par, 1, HALF * half + h, :],
                                           pr[:, h * P:h * P + P], start=False, stop=True, skip_group_check=True)
                mm.then_inc(pv_mm, 1)

            def transpose_x(st, b, par):
                pe.wait_ge(xn_ready, b + 1)
                dst = take(st, "B", "xT")
                for k in range(KT):
                    for t in range(TB):
                        mm = pe.transpose(dst[:, k * S + t * P:k * S + t * P + P], xn[:, par, t, k * P:k * P + P], ident[:])
                mm.then_inc(xT_mm, 1)

            def project_qk(st, b, par, qk, bk):
                j = "qk".index(qk)
                pe.wait_ge(xT_ready, b + 1)
                dst = take(st, bk, qk)
                for m in range(KT):
                    for k in range(KT):
                        col = j * D + m * P
                        mm = pe.matmul(dst[:, m * S:m * S + S], wqk_sb[:, k, col:col + P], xT[:, par, k, :],
                                       start=(k == 0), stop=(k == KT - 1))
                mm.then_inc((q_mm, k_mm)[j], 1)

            def tokens_by(dst, lhsT, rhs):
                for t in range(TB):
                    for k in range(KT):
                        mm = pe.matmul(dst[:, t * D:t * D + D], lhsT[:, k, t * P:t * P + P], rhs[:, k, :],
                                       start=(k == 0), stop=(k == KT - 1))
                return mm

            def transpose_max(st, b, half, bk):
                pe.wait_ge(neg_step, 6 * (2 * b + half) + 6)
                dst = take(st, bk, f"max_h{half}").ap().bitcast(BF16)
                for t in range(TB):
                    mm = pe.transpose(dst[0:PARTS * HALF, t * P:t * P + P],
                                      neg_parts[:, half, t].rearrange("p r h -> p (r h)"), ident_bf[:])
                mm.then_inc(max_mm, 1)

            def suffix(st, b, par, half):
                pe.wait_ge(v_ready, b + 1)
                dst = take(st, "B", f"suffix{half}")
                heads = slice(HALF * half, HALF * half + HALF)
                w = HALF * NVC
                pe.matmul(dst[:, 0:w], later[:], v_sb[:, par, 0, heads, 0:NVC], start=True, stop=False)
                pe.matmul(dst[:, 0:w], ones[:], v_sb[:, par, 1, heads, 0:NVC], start=False, stop=True)
                pe.matmul(dst[:, w:2 * w], later[:], v_sb[:, par, 1, heads, 0:NVC], start=True, stop=True).then_inc(suffix_mm, 1)

            def transpose_o(st, b, half, bk):
                pe.wait_ge(o_raw_ready, 2 * b + half + 1)
                dst = take(st, bk, f"o{half}")
                for t in range(TB):
                    for g in range(2):
                        at = (2 * t + g) * P
                        mm = pe.transpose(dst[:, at:at + P], o_raw[:, half, g, t * P:t * P + P], ident[:])
                mm.then_inc(o_mm, 1)

            def transpose_norm_o(st, b, half):
                pe.wait_ge(norm_step, 3 * (2 * b + half) + 3)
                dst = take(st, "A", f"norm_o{half}")
                for t in range(TB):
                    mm = pe.transpose(dst[:, t * P:t * P + P], o_tok[:, half, t, :], ident[:])
                mm.then_inc(oT_mm, 1)

            pe.wait_ge(const_ready, 1)
            transpose_x(Step(-2, -2), 0, 0)
            pe.wait_ge(bqk_ready, 1)
            pe.transpose(ps1[:, 0:2 * KT], bqk_ordered[:], ident[0:2 * KT, 0:2 * KT]).then_inc(bqk_mm, 1)
            pe.wait_ge(w_ordered, 1)
            for b in range(2):
                st = Step(b - 2, b - 2)
                if b > 0:
                    transpose_x(st, b, b)
                project_qk(st, b, b, "q", "B")
                project_qk(st, b, b, "k", "A")
            pe.wait_ge(w8_ready, 1)
            for k in range(KT):
                for o in range(KT):
                    mm = pe.transpose(ps2[:].bitcast(BF16)[:, k * D + o * P:k * D + o * P + P], w8_bf[:, o, k * P:k * P + P], ident_bf[:])
            mm.then_inc(w8_mm, 1)
            pe.wait_ge(w8T_ready, 1)
            pe.wait_ge(mask_landed, MASK_DMAS * 16)
            pe.wait_ge(const_ready, CONSTS)
            pe.wait_ge(wv_landed, 2 * 16)
            pe.wait_ge(proj_landed, 2 * 16)

            def run(st):
                n, p = st.n, st.par
                for i in range(SLOTS):
                    if st.has(1):
                        phase1(n + 1, 1 - p, i)
                    if st.has(0):
                        phase2(n, p, i)
                    if i > 0 and st.has(0):
                        values(n, p, i - 1)
                    if i == 0 and st.has(-1):
                        values(n - 1, 1 - p, SLOTS - 1)
                    if i == 0:
                        if st.has(-1):
                            transpose_norm_o(st, n - 1, 0)
                        if st.has(2):
                            transpose_x(st, n + 2, p)
                    elif i == 1:
                        if st.has(0):
                            transpose_max(st, n, 1, "A")
                        if st.has(2):
                            project_qk(st, n + 2, p, "q", "B")
                    elif i == 2:
                        if st.has(2):
                            project_qk(st, n + 2, p, "k", "A")
                        if st.has(-1):
                            suffix(st, n - 1, 1 - p, 1)
                    elif i == 3:
                        if st.has(-1):
                            transpose_o(st, n - 1, 1, "A")
                        if st.has(1):
                            pe.wait_ge(xT_ready, n + 2)
                            tokens_by(take(st, "B", "v"), xT[:, 1 - p], wqkv_sb[:, :, 2 * D:]).then_inc(v_mm, 1)
                        if st.has(0):
                            pe.wait_ge(quant_pool, 2 * n + 2)
                            tokens_by(take(st, "A", "ffn"), xq[:, p], w8T[:]).then_inc(ffn_mm, 1)
                    elif i == 4:
                        if st.has(0):
                            suffix(st, n, p, 0)
                        if st.has(-1):
                            transpose_norm_o(st, n - 1, 1)
                        if st.has(1):
                            transpose_max(st, n + 1, 0, "B")
                    else:
                        if st.has(0):
                            transpose_o(st, n, 0, "B")
                        if st.has(-1):
                            pe.wait_ge(oT_ready, 2 * n)
                            tokens_by(take(st, "A", "proj"), oT[:], wo_sb[:]).then_inc(proj_mm, 1)

            all_steps(pe, run)


_INS = ["L0_attn_x", "L0_attn_Wqkv", "L0_attn_bqkv", "L0_attn_Wo", "L0_attn_bo", "L0_ffn_weight",
        "L0_ffn_weight_scale", "L0_ffn_input_scale"]


def kernel(**inputs):
    import numpy as _np
    import concourse.bacc as _bacc
    from concourse import mybir as _mybir
    from concourse.bass_utils import run_bass_kernel_spmd as _run

    nc = _bacc.Bacc("TRN2", target_bir_lowering=False, num_devices=1)
    arrays, args = {}, []
    for name in _INS:
        a = _np.ascontiguousarray(inputs[name])
        arrays[f"in_{name}_dram"] = a
        args.append(nc.dram_tensor(f"in_{name}_dram", a.shape, _mybir.dt.from_np(a.dtype), kind="ExternalInput").ap())
    args.append(nc.dram_tensor("out_0_dram", (B, S, D), _mybir.dt.float32, kind="ExternalOutput").ap())
    build(nc, *args)
    r = _run(nc, [arrays], core_ids=[0])
    return r.results[0]["out_0_dram"]
```

```python
from contextlib import ExitStack

import concourse.bass as bass
from concourse import mybir

ALU = mybir.AluOpType
ACT = mybir.ActivationFunctionType
AX_X = mybir.AxisListType.X
BF16 = mybir.dt.bfloat16
FP16 = mybir.dt.float16
F32 = mybir.dt.float32
I32 = mybir.dt.int32
U8 = mybir.dt.uint8
U16 = mybir.dt.uint16

P = 128
B = 8
S = 256
D = 256
H = 16
HD = D // H
TB = S // P
KT = D // P
HALF = H // 2
SLOTS = 6
EPS = 1e-5
SCALE = HD ** -0.5
MASKED = -10000.0 / SCALE
FP8_MAX = 448.0

PARTS = 3
Q_BLOCKS = (0, 0, 1, 2)
K_BLOCKS = (2, 1, 0, 0)
RUN = 3 * HD
PROD = 2 * RUN
Q_READ = 112
ROW_MAX = PROD
ROW_MASK = PROD + PARTS
MB = 5
MASK_ROWS = -(-P // MB)
K_SOFT = PROD + PARTS
K_MAX = ROW_MASK + MASK_ROWS
G = 2.0 ** 24
MASK_C = 16.0
NVC = HD + 1

USES = {
    "A": [("norm_o0", -1), ("max_h1", 0), ("k", 2), ("o1", -1), ("ffn", 0), ("norm_o1", -1), ("proj", -1)],
    "B": [("xT", 2), ("q", 2), ("suffix1", -1), ("v", 1), ("suffix0", 0), ("max_h0", 1), ("o0", 0)],
}
EARLY = B - 2
USES_BEFORE = {"A": [("k", 0), ("k", 1)], "B": [("xT", 0), ("q", 0), ("xT", 1), ("q", 1), ("v", 0)]}
FIRST, LAST = -1, B + 1
LOOP = range(2, 6)


class Step:

    def __init__(self, n, like):
        self.n, self.like, self.par = n, like, like % 2

    def has(self, off):
        return 0 <= self.like + off < B

    def uses(self, bank):
        uses = [(who, off) for who, off in USES[bank]
                if self.has(off) and (who, self.like + off) not in USES_BEFORE[bank]]
        if bank == "A" and self.like == EARLY + 1:
            uses.remove(("max_h1", 0))
        return uses

    def does(self, name):
        return name in [who for bank in "AB" for who, _ in self.uses(bank)]

    def use_before(self, bank, name):
        uses = self.uses(bank)
        at = [who for who, _ in uses].index(name)
        if at:
            return uses[at - 1][0], self.n + uses[at - 1][1]
        for back in range(1, self.like - FIRST + 1):
            uses = Step(self.n, self.like - back).uses(bank)
            if uses:
                return uses[-1][0], self.n - back + uses[-1][1]
        return USES_BEFORE[bank][-1]


def all_steps(eng, run):
    for n in range(FIRST, LOOP.start):
        run(Step(n, n))
    with eng.Fori(0, len(LOOP) // 2) as turn:
        n = turn * 2 + LOOP.start
        run(Step(n, LOOP.start))
        run(Step(n + 1, LOOP.start + 1))
    for n in range(LOOP.stop, LAST + 1):
        run(Step(n, n))


def wait(eng, sem, value, passed=None):
    if not isinstance(value, int) or value > 0:
        eng.wait_ge(sem, value)
        if not isinstance(value, int) and passed is not None:
            eng.sem_inc(passed, 1)


def build(nc, x, wqkv, bqkv, wo, bo, w8, w8_scale, in_scale, out):
    ctx = ExitStack()
    with ctx:
        def sb(name, shape, dt=F32):
            return ctx.enter_context(nc.sbuf_tensor(name, shape, dt))

        def psum(name, shape, dt=F32):
            return ctx.enter_context(nc.psum_tensor(name, shape, dt))

        def sem(name):
            return ctx.enter_context(nc.semaphore(name))

        ident = sb("ident", [P, P])
        ident_bf = sb("ident_bf", [P, P], BF16)
        later = sb("later", [P, P])
        ones = sb("ones", [P, P])
        fixed_q = sb("fixed_q", [PARTS + MASK_ROWS, TB, P], BF16)
        fixed_k = sb("fixed_k", [PARTS + MASK_ROWS, TB, P], BF16)
        neg_floor = sb("neg_floor", [P, TB, HALF])
        wqkv_sb = sb("wqkv_sb", [P, KT, 3 * D])
        wqk_sb = sb("wqk_sb", [P, KT, 2 * D])
        wo_sb = sb("wo_sb", [P, KT, D])
        bqk_row = sb("bqk_row", [2 * KT, P])
        bqk_ordered = sb("bqk_ordered", [2 * KT, P])
        bqk_col = sb("bqk_col", [P, 2 * KT])
        bv_all = sb("bv_all", [P, D])
        bo_all = sb("bo_all", [P, D])
        bv_T = sb("bv_T", [P, KT, P])
        out_bias = sb("out_bias", [P, D])
        w8_raw = sb("w8_raw", [P, KT, D], U8)
        w8_wide = sb("w8_wide", [P, KT, D], U16)
        w8_mag = sb("w8_mag", [P, KT, D], U16)
        w8_sign = sb("w8_sign", [P, KT, D], U16)
        w8_bits = sb("w8_bits", [P, KT, D], U16)
        w8_bf = sb("w8_bf", [P, KT, D], BF16)
        w8T = sb("w8T", [P, KT, D], BF16)
        in_scale_bf = sb("in_scale_bf", [P, 1], BF16)
        in_scale_f = sb("in_scale_f", [P, 1])
        w8_scale_f = sb("w8_scale_f", [P, 1])
        inv_in_scale = sb("inv_in_scale", [P, 1])
        ffn_scale = sb("ffn_scale", [P, 1])

        NT = B * TB
        x_all = sb("x_all", [P, NT, D])
        stats = sb("stats", [P, NT, 6])
        mean_var = sb("mean_var", [P, NT, 2])
        var_eps = sb("var_eps", [P, NT])
        std = sb("std", [P, NT])
        rstd0 = sb("rstd0", [P, NT])
        rstd_sq = sb("rstd_sq", [P, NT])
        rstd_e = sb("rstd_e", [P, NT])
        rstd_f = sb("rstd_f", [P, NT])
        rstd = sb("rstd", [P, NT])
        xn = sb("xn", [P, 2, TB, D])

        xT = sb("xT", [P, 2, KT, S])
        x_over = sb("x_over", [P, KT, S])
        x_clip = sb("x_clip", [P, 2, KT, S])
        x_exp = sb("x_exp", [P, KT, S])
        x_big = sb("x_big", [P, 2, KT, S])
        x_sum = sb("x_sum", [P, KT, S])
        xq = sb("xq", [P, 2, KT, S], BF16)
        parts = {qk: sb(f"{qk}_parts", [P, 2, PARTS, KT, S], BF16) for qk in "qk"}
        rest = {qk: sb(f"{qk}_rest", [P, KT, S]) for qk in "qk"}
        q_stack = sb("q_stack", [P, 2, H, S], BF16)
        k_stack = sb("k_stack", [P, 2, H, S], BF16)
        v_sb = sb("v_sb", [P, 2, TB, H, 32])
        row_max = sb("row_max", [P, 2, TB, HALF])
        neg_max = sb("neg_max", [P, 2, TB, HALF])
        neg_r1 = sb("neg_r1", [P, 2, TB, HALF])
        neg_parts = sb("neg_parts", [P, 2, TB, PARTS, HALF], BF16)
        e_arg = sb("e_arg", [P, 2, TB, HALF])
        e_sb = sb("e_sb", [P, 2, 2, TB, HALF])
        max_rows = sb("max_rows", [PARTS * HALF, 2, S], BF16)
        probs = sb("probs", [P, 2, 1024])
        o_raw = sb("o_raw", [P, 2, 2, S])
        o_masked = sb("o_masked", [P, 2, H, NVC])
        o_sum = sb("o_sum", [P, 2, H, NVC])
        o_den = sb("o_den", [P, 2, H])
        o_tok = sb("o_tok", [P, 2, TB, P])
        oT = sb("oT", [P, 2, KT, S])
        xb = sb("xb", [P, TB, D])
        y1 = sb("y1", [P, 2, TB, D])
        y = sb("y", [P, 2, TB, D])

        q_rows = HD * len(Q_BLOCKS) + Q_READ - PROD
        scratch = {qk: nc.dram_tensor(f"{qk}_scratch", (2, 2, rows, HALF, S), BF16, kind="Internal").ap()
                   for qk, rows in (("q", q_rows), ("k", HD * len(K_BLOCKS)))}
        ps1 = psum("ps1", [P, 1024])
        ps2 = psum("ps2", [P, 1024])
        pso = psum("pso", [P, 2, 2, S])
        bank = {"A": psum("bankA", [P, 512]), "B": psum("bankB", [P, 512])}

        AT = {"q": (0, 1, 2), "k": (2, 1, 0)}

        x_landed = [sem(f"x{g}_landed") for g in range(3)]
        w_landed, bqk_landed, ffn_landed = sem("w_landed"), sem("bqk_landed"), sem("ffn_landed")
        wv_landed, proj_landed = sem("wv_landed"), sem("proj_landed")
        passed = sem("passed")
        floor_ready = sem("floor_ready")
        const_ready, pool_chain = sem("const_ready"), sem("pool_chain")
        w_ordered = sem("w_ordered")
        fixed_landed = [sem(f"fixed{par}_landed") for par in range(2)]
        init_dve = sem("init_dve")
        bqk_ready, bqk_mm, bqk_col_ready = sem("bqk_ready"), sem("bqk_mm"), sem("bqk_col_ready")
        v_ones_ready = sem("v_ones_ready")
        bias_mm, bv_T_ready, out_bias_ready = sem("bias_mm"), sem("bv_T_ready"), sem("out_bias_ready")
        std_ready = sem("std_ready")
        dve_chain, w8_mm, w8T_ready = sem("dve_chain"), sem("w8_mm"), sem("w8T_ready")
        w8_ready = sem("w8_ready")
        xn_ready, xT_mm, xT_ready = sem("xn_ready"), sem("xT_mm"), sem("xT_ready")
        q_mm, k_mm, v_mm = sem("q_mm"), sem("k_mm"), sem("v_mm")
        part1_ready, rest_ready = sem("part1_ready"), sem("rest_ready")
        part2_ready, split_ready = sem("part2_ready"), sem("split_ready")
        spilled = [sem(f"{qk}_spilled") for qk in "qk"]
        stack_landed = [sem(f"stack_landed{h}") for h in range(2)]
        v_ready = sem("v_ready")
        ph1_mm, max_done = sem("ph1_mm"), sem("max_done")
        neg_step, max_mm, max_rows_ready = sem("neg_step"), sem("max_mm"), sem("max_rows_ready")
        max_landed = [sem(f"max_landed{h}") for h in range(2)]
        e_ready = sem("e_ready")
        ph2_mm, exp_done, causal_done, pv_mm = sem("ph2_mm"), sem("exp_done"), sem("causal_done"), sem("pv_mm")
        o_raw_ready, o_mm, suffix_mm = sem("o_raw_ready"), sem("o_mm"), sem("suffix_mm")
        masked_ready, norm_step = sem("masked_ready"), sem("norm_step")
        oT_mm, oT_ready = sem("oT_mm"), sem("oT_ready")
        quant_dve, quant_pool = sem("quant_dve"), sem("quant_pool")
        ffn_mm, xb_ready, y1_ready = sem("ffn_mm"), sem("xb_ready"), sem("y1_ready")
        proj_mm, y_ready = sem("proj_mm"), sem("y_ready")
        out_landed = [sem(f"out_landed{p}") for p in range(2)]
        read = {"xT": (xT_ready, 1, 1), "q": (rest_ready, 2, 1), "k": (rest_ready, 2, 2),
                "v": (v_ready, 1, 1), "max_h0": (max_rows_ready, 2, 1), "max_h1": (max_rows_ready, 2, 2),
                "suffix0": (masked_ready, 2, 1), "suffix1": (masked_ready, 2, 2),
                "o0": (norm_step, 6, 1), "o1": (norm_step, 6, 4),
                "norm_o0": (oT_ready, 2, 1), "norm_o1": (oT_ready, 2, 2),
                "ffn": (y1_ready, 1, 1), "proj": (y_ready, 1, 1)}

        STACK_DMAS = 4
        SPILL_DMAS = 4
        WARM_UP = 18
        CONSTS = 3
        X_GROUPS = ((0, TB), (TB, 2 * TB), (2 * TB, B * TB))

        def split(eng, b, par, qk):
            j = "qk".index(qk)
            pt, r = parts[qk], rest[qk]
            wait(eng, rest_ready, 2 * b + j + 1, passed)
            eng.tensor_scalar(pt[:, par, AT[qk][1]], r[:], 1.0, 1.0, ALU.mult, ALU.mult).then_inc(part2_ready, 1)
            wait(eng, part2_ready, 2 * b + j + 1, passed)
            eng.tensor_tensor(pt[:, par, AT[qk][2]], r[:], pt[:, par, AT[qk][1]], ALU.subtract).then_inc(split_ready, 1)

        x_tok = x.rearrange("b (t p) d -> p (b t) d", p=P)
        block = ctx.enter_context(nc.Block())

        @block.sync
        def _(sp):
            def load_x(g):
                lo, hi = X_GROUPS[g]
                sp.dma_start(x_all[:, lo:hi, :], x_tok[:, lo:hi, :]).then_inc(x_landed[g], 16)

            def load_fixed(par, places):
                for dst, rows in places:
                    r, heads = rows.shape[0], dst.shape[1]
                    sp.dma_start(dst, rows.rearrange("r t p -> r (t p)").unsqueeze(1).to_broadcast([r, heads, S])).then_inc(fixed_landed[par], 16)

            def fixed_in_stacks(par):
                load_fixed(par, [(k_stack[ROW_MAX:K_MAX, par], fixed_k[:]), (q_stack[Q_READ:K_MAX, par], fixed_q[again:])])

            for par in range(2):
                sp.sem_inc(out_landed[par], 16)

            w_in = wqkv.rearrange("(k p) n -> p k n", p=P)
            load_x(0)
            sp.dma_start(wqkv_sb[:, :, 0:2 * D], w_in[:, :, 0:2 * D]).then_inc(w_landed, 16)
            sp.dma_start(bqk_row[:], bqkv[0:2 * D].rearrange("(m p) -> m p", p=P)).then_inc(bqk_landed, 16)
            load_x(1)
            for t, src in ((in_scale_bf[:], in_scale.partition_broadcast(P)),
                           (w8_scale_f[:], w8_scale.partition_broadcast(P)),
                           (w8_raw[:], w8.bitcast(U8).rearrange("(k p) n -> p k n", p=P))):
                sp.dma_start(t, src).then_inc(ffn_landed, 16)
            sp.dma_start(wqkv_sb[:, :, 2 * D:], w_in[:, :, 2 * D:]).then_inc(wv_landed, 16)
            sp.dma_start(bv_all[:], bqkv[2 * D:3 * D].partition_broadcast(P)).then_inc(wv_landed, 16)
            load_x(2)
            sp.dma_start(bo_all[:], bo.partition_broadcast(P)).then_inc(proj_landed, 16)
            sp.dma_start(wo_sb[:], wo.rearrange("(k p) n -> p k n", p=P)).then_inc(proj_landed, 16)
            again = Q_READ - ROW_MAX
            sp.wait_ge(const_ready, CONSTS)
            load_fixed(0, [(scratch["q"][par, half, HD * len(Q_BLOCKS):], fixed_q[0:again])
                           for par in range(2) for half in range(2)])
            fixed_in_stacks(0)

            def spill(b, par, qk, first):
                j = "qk".index(qk)
                if first:
                    wait(sp, part1_ready, 2 * b + j + 1, passed)
                    for half in range(2):
                        wait(sp, stack_landed[half], 16 * STACK_DMAS * (b - 1), passed)
                else:
                    wait(sp, split_ready, 2 * b + j + 1, passed)
                blocks = (Q_BLOCKS, K_BLOCKS)[j]
                at = [i for i, part in enumerate(blocks) if (part == 0) == first]
                src = parts[qk][:, par, AT[qk][0]] if first else parts[qk][:, par, 1:3] if qk == "q" else parts[qk][:, par, 0:2]
                for half in range(2):
                    rows = scratch[qk][par, half, HD * at[0]:HD * at[-1] + HD]
                    s = src[:, half].unsqueeze(1).to_broadcast([P, 2, S]) if first else src[:, :, half]
                    sp.dma_start(rows.rearrange("(i d) h t -> (d h) i t", i=2), s).then_inc(spilled[j], 16)

            def stack(b, par, half):
                wait(sp, ph2_mm, SLOTS * (b - 2) + 3 * half + 3, passed)
                heads = slice(HALF * half, HALF * half + HALF)
                for j, (stack_sb, qk, runs) in enumerate(((q_stack, "q", ((0, 0, RUN), (RUN, HD, Q_READ - RUN))),
                                                          (k_stack, "k", ((0, HD, RUN), (RUN, 0, RUN))))):
                    wait(sp, spilled[j], 16 * SPILL_DMAS * (b + 1), passed)
                    for to, at, rows in runs:
                        sp.dma_start(stack_sb[to:to + rows, par, heads, :],
                                     scratch[qk][par, half, at:at + rows]).then_inc(stack_landed[half], 16)

            def max_to_stack(b, par, half):
                wait(sp, max_rows_ready, 2 * b + half + 1, passed)
                sp.dma_start(q_stack[ROW_MAX:ROW_MASK, par, HALF * half:HALF * half + HALF, :],
                             max_rows[:, half, :]).then_inc(max_landed[half], 16)

            def run(st):
                n, p = st.n, st.par
                if st.like == EARLY + 1:
                    max_to_stack(n, p, 1)
                if st.has(-2):
                    wait(sp, y_ready, n - 1, passed)
                    sp.dma_start(out[bass.ds(n - 2, 1)].rearrange("b (t p) d -> p (b t) d", p=P),
                                 y[:, p]).then_inc(out_landed[p], 16)
                if st.does("max_h1"):
                    max_to_stack(n, p, 1)
                if st.does("xT"):
                    for first in (True, False):
                        spill(n + 2, p, "q", first)
                        spill(n + 2, p, "k", first)
                    stack(n + 2, p, 0)
                if st.has(1):
                    max_to_stack(n + 1, 1 - p, 0)
                if st.does("xT") or st.like == FIRST:
                    stack(n + 2, p, 1)

            def spill_qk(b, par, first):
                for qk in "qk":
                    spill(b, par, qk, first)

            spill_qk(0, 0, True)
            spill_qk(0, 0, False)
            sp.wait_ge(fixed_landed[0], 6 * 16)
            stack(0, 0, 0)
            spill_qk(1, 1, True)
            stack(0, 0, 1)
            spill_qk(1, 1, False)
            fixed_in_stacks(1)
            stack(1, 1, 0)
            all_steps(sp, run)
            for par in range(2):
                sp.wait_ge(out_landed[par], 16 + 16 * B // 2)

        @block.gpsimd
        def _(pool):
            steps = [0]

            def link(ins):
                steps[0] += 1
                ins.then_inc(pool_chain, 1)
                pool.wait_ge(pool_chain, steps[0])

            pool.memset(ident[:], 0.0)
            pool.memset(later[:], 1.0)
            pool.memset(ones[:], 1.0)
            pool.memset(fixed_q[:], 0.0)
            link(pool.memset(fixed_k[:], 0.0))
            link(pool.affine_select(out=ident[:], in_=ident[:], compare_op=ALU.not_equal, fill=1.0,
                                    base=0, pattern=[[-1, P]], channel_multiplier=1))
            pool.tensor_copy(ident_bf[:], ident[:]).then_inc(const_ready, 1)
            link(pool.memset(fixed_k[0:PARTS], 1.0))
            link(pool.affine_select(out=fixed_q[:], in_=fixed_q[:], compare_op=ALU.is_ge, fill=G,
                                    base=MB * PARTS, pattern=[[0, TB], [1, P]], channel_multiplier=-MB))
            for j in range(MB):
                link(pool.affine_select(out=fixed_q[:], in_=fixed_q[:], compare_op=ALU.not_equal, fill=G ** -j,
                                        base=MB * PARTS - j, pattern=[[0, TB], [1, P]], channel_multiplier=-MB))
                ins = pool.affine_select(out=fixed_k[:], in_=fixed_k[:], compare_op=ALU.not_equal,
                                         fill=-MASK_C * G ** j,
                                         base=MB * PARTS - j, pattern=[[0, TB], [1, P]], channel_multiplier=-MB)
                if j < MB - 1:
                    link(ins)
            ins.then_inc(const_ready, 1)
            pool.affine_select(out=later[:], in_=later[:], compare_op=ALU.is_gt, fill=0.0,
                               base=0, pattern=[[-1, P]], channel_multiplier=1).then_inc(const_ready, 1)
            link(pool.memset(neg_floor[:], -MASKED))
            pool.affine_select(out=neg_floor[:, TB - 1], in_=neg_floor[:, TB - 1], compare_op=ALU.not_equal,
                               fill=3.0e38, base=-(P - 1), pattern=[[0, HALF]],
                               channel_multiplier=1).then_inc(floor_ready, 1)
            pool.memset(v_sb[:], 1.0).then_inc(v_ones_ready, 1)
            pool.wait_ge(floor_ready, 1)
            pool.wait_ge(v_ones_ready, 1)

            def causal(b, i):
                c = SLOTS * b + i
                wait(pool, exp_done, c + 1, passed)
                pr = probs[:, i % 2, :]
                if i % 3 < 2:
                    v, heads = pr.rearrange("p (h t) -> p h t", h=4)[:, :, 0:P], 4
                else:
                    v, heads = pr.rearrange("p (h t) -> p h t", h=HALF), HALF
                pool.affine_select(out=v, in_=v, compare_op=ALU.is_ge, fill=0.0, base=0,
                                   pattern=[[0, heads], [1, P]], channel_multiplier=-1).then_inc(causal_done, 1)

            def round_x(b, par):
                wait(pool, quant_dve, 4 * b + 4, passed)
                pool.tensor_tensor(x_sum[:], x_clip[:, par], x_big[:, par], ALU.add).then_inc(quant_pool, 1)
                wait(pool, quant_pool, 2 * b + 1, passed)
                wait(pool, ffn_mm, b - 1, passed)
                pool.tensor_tensor(xq[:, par], x_sum[:], x_big[:, par], ALU.subtract).then_inc(quant_pool, 1)

            def residual(b):
                wait(pool, y1_ready, b, passed)
                pool.tensor_tensor(xb[:], x_all[:, bass.ds(TB * b, TB), :],
                                   out_bias[:].unsqueeze(1).to_broadcast([P, TB, D]),
                                   ALU.add).then_inc(xb_ready, 1)

            def run(st):
                n, p = st.n, st.par
                if st.has(0):
                    causal(n, 0)
                    causal(n, 1)
                    if st.like == 0:
                        round_x(0, 0)
                        pool.wait_ge(out_bias_ready, 1)
                        for g in range(3):
                            pool.wait_ge(x_landed[g], 16)
                        residual(0)
                    causal(n, 2)
                if st.does("xT"):
                    split(pool, n + 2, p, "q")
                    split(pool, n + 2, p, "k")
                if st.has(0):
                    causal(n, 3)
                if st.has(1) and st.like > FIRST:
                    round_x(n + 1, 1 - p)
                if st.has(0):
                    causal(n, 4)
                if st.has(1) and st.like > FIRST:
                    residual(n + 1)
                if st.has(0):
                    causal(n, 5)

            pool.wait_ge(split_ready, 2)
            for qk in "qk":
                split(pool, 1, 1, qk)
            all_steps(pool, run)

        @block.scalar
        def _(act):
            def square_roots(g):
                lo, hi = X_GROUPS[g]
                act.wait_ge(init_dve, 2 * g + 1)
                act.activation(std[:, lo:hi], var_eps[:, lo:hi], ACT.Sqrt).then_inc(std_ready, 1)

            def exponentials(st, b, i):
                c = SLOTS * b + i
                act.wait_ge(ph2_mm, c + 1)
                wait(act, pv_mm, c - 1)
                ps = ps1 if st.like == B - 1 and i % 2 else ps2
                act.activation(probs[:, i % 2, :], ps[:], ACT.Exp, scale=SCALE).then_inc(exp_done, 1)

            def part1(b, par, qk, bk):
                j = "qk".index(qk)
                act.wait_ge((q_mm, k_mm)[j], b + 1)
                wait(act, spilled[j], 16 * SPILL_DMAS * (b - 1))
                for half in range(2):
                    ins = act.activation(parts[qk][:, par, AT[qk][0], half, :], bank[bk][:, half * S:half * S + S],
                                         ACT.Identity, bias=bqk_col[:, KT * j + half:KT * j + half + 1])
                ins.then_inc(part1_ready, 1)

            def values_out(b, par):
                act.wait_ge(v_mm, b + 1)
                wait(act, pv_mm, SLOTS * (b - 1))
                wait(act, suffix_mm, 2 * b - 2)
                act.activation(v_sb[:, par, :, :, 0:HD], bank["B"][:].rearrange("p (t h d) -> p t h d", t=TB, h=H),
                               ACT.Copy).then_inc(v_ready, 1)

            def o_out(b, half):
                c = 2 * b + half
                act.wait_ge(pv_mm, SLOTS * b + 3 * half + 3)
                wait(act, o_mm, c - 1)
                act.activation(o_raw[:, half], pso[:, half], ACT.Copy).then_inc(o_raw_ready, 1)

            def oT_out(st, b, half, bk):
                c = 2 * b + half
                act.wait_ge(oT_mm, c + 1)
                wait(act, proj_mm, b - 1)
                src = (ps1[:, 512:512 + S], ps2[:, 0:S])[half] if st.like == B else bank[bk][:, 0:S]
                act.activation(oT[:, 1 - st.par, half], src, ACT.Copy).then_inc(oT_ready, 1)

            def max_out(b, par, half, bk):
                c = 2 * b + half
                act.wait_ge(neg_step, SLOTS * c + 6)
                wait(act, masked_ready, c - 3)
                act.activation(e_sb[:, par, half], e_arg[:, half], ACT.Exp, scale=SCALE).then_inc(e_ready, 1)
                act.wait_ge(max_mm, c + 1)
                wait(act, max_landed[half], 16 * b)
                src = bank[bk].ap() if bk else ps1[:]
                act.activation(max_rows[:, half, :], src.bitcast(BF16)[0:PARTS * HALF, 0:S],
                               ACT.Copy).then_inc(max_rows_ready, 1)

            def xT_out(b, par):
                act.wait_ge(xT_mm, b + 1)
                wait(act, v_mm, b - 1)
                wait(act, quant_dve, 4 * (b - 2) + 1)
                act.activation(xT[:, par], bank["B"][:].rearrange("p (k s) -> p k s", k=KT), ACT.Copy).then_inc(xT_ready, 1)

            def run(st):
                n, p = st.n, st.par
                if st.has(0):
                    exponentials(st, n, 0)
                if st.has(-1):
                    o_out(n - 1, 1)
                    oT_out(st, n - 1, 0, "A")
                if st.does("xT"):
                    xT_out(n + 2, p)
                if st.has(0):
                    exponentials(st, n, 1)
                if st.does("max_h1"):
                    max_out(n, p, 1, "A")
                if st.does("xT"):
                    part1(n + 2, p, "q", "B")
                if st.has(0):
                    exponentials(st, n, 2)
                if st.does("xT"):
                    part1(n + 2, p, "k", "A")
                if st.has(0):
                    exponentials(st, n, 3)
                    o_out(n, 0)
                if st.does("v"):
                    values_out(n + 1, 1 - p)
                if st.has(0):
                    exponentials(st, n, 4)
                if st.like == B - 1:
                    exponentials(st, n, 5)
                if st.has(-1):
                    oT_out(st, n - 1, 1, "A")
                if st.has(1):
                    max_out(n + 1, 1 - p, 0, "B")
                if st.has(0) and st.has(1):
                    exponentials(st, n, 5)
                if st.like == EARLY:
                    max_out(n + 1, 1 - p, 1, None)

            square_roots(0)
            act.wait_ge(w_landed, 16)
            for k in range(KT):
                ins = act.activation(wqk_sb[:, k].rearrange("p (m d h) -> p m d h", m=2 * KT, d=HD),
                                     wqkv_sb[:, k, 0:2 * D].rearrange("p (m h d) -> p m d h", m=2 * KT, d=HD), ACT.Copy)
            ins.then_inc(w_ordered, 1)
            for b in range(2):
                xT_out(b, b)
                if b == 0:
                    square_roots(1)
                    act.wait_ge(bqk_col_ready, 1)
                part1(b, b, "q", "B")
                part1(b, b, "k", "A")
            act.wait_ge(v_ones_ready, 1)
            values_out(0, 0)
            square_roots(2)
            all_steps(act, run)

        @block.vector
        def _(dve):
            steps = [0]

            def link(ins, s=dve_chain):
                steps[0] += 1
                ins.then_inc(s, 1)
                dve.wait_ge(s, steps[0])

            def moments(lo, hi):
                for t in range(lo, hi):
                    ins = dve.bn_stats(stats[:, t, :], x_all[:, t, :])
                return ins

            def variances(g):
                lo, hi = X_GROUPS[g]
                for t in range(lo, hi):
                    ins = dve.bn_aggr(mean_var[:, t, :], stats[:, t, :])
                link(ins)
                dve.tensor_scalar(var_eps[:, lo:hi], mean_var[:, lo:hi, 1], EPS, None, ALU.add).then_inc(init_dve, 1)

            def inverse_std(g):
                lo, hi = X_GROUPS[g]
                dve.wait_ge(std_ready, g + 1)
                link(dve.reciprocal(rstd0[:, lo:hi], std[:, lo:hi]))
                link(dve.tensor_tensor(rstd_sq[:, lo:hi], rstd0[:, lo:hi], rstd0[:, lo:hi], ALU.mult))
                link(dve.tensor_tensor(rstd_e[:, lo:hi], rstd_sq[:, lo:hi], var_eps[:, lo:hi], ALU.mult))
                link(dve.tensor_scalar(rstd_f[:, lo:hi], rstd_e[:, lo:hi], -0.5, 1.5, ALU.mult, ALU.add))
                dve.tensor_tensor(rstd[:, lo:hi], rstd0[:, lo:hi], rstd_f[:, lo:hi], ALU.mult).then_inc(init_dve, 1)
                dve.wait_ge(init_dve, 2 * g + 2)

            def normalise(b, par):
                wait(dve, xT_mm, b - 1)
                for t in range(TB):
                    i = TB * b + t
                    ins = dve.tensor_scalar(xn[:, par, t, :], x_all[:, bass.ds(i, 1), :].rearrange("p t d -> p (t d)"),
                                            mean_var[:, bass.ds(i, 1), 0], rstd[:, bass.ds(i, 1)],
                                            ALU.subtract, ALU.mult)
                ins.then_inc(xn_ready, 1)

            def scales():
                dve.wait_ge(ffn_landed, 3 * 16)
                link(dve.tensor_copy(in_scale_f[:], in_scale_bf[:]))
                dve.tensor_tensor(ffn_scale[:], in_scale_f[:], w8_scale_f[:], ALU.mult)
                link(dve.reciprocal(inv_in_scale[:], in_scale_f[:]))

            def fp8_weight_fields():
                link(dve.tensor_copy(w8_wide[:], w8_raw[:]))
                dve.tensor_scalar(w8_mag[:], w8_wide[:], 0x7F, 7, ALU.bitwise_and, ALU.logical_shift_left)
                link(dve.tensor_scalar(w8_sign[:], w8_wide[:], 0x80, 8, ALU.bitwise_and, ALU.logical_shift_left))

            def fp8_weight():
                link(dve.tensor_tensor(w8_bits[:], w8_mag[:], w8_sign[:], ALU.bitwise_or))
                dve.tensor_scalar(w8_bf[:], w8_bits[:].bitcast(FP16), 256.0, None, ALU.mult).then_inc(w8_ready, 1)

            def clip_x(b, par):
                dve.wait_ge(xT_ready, b + 1)
                dve.tensor_scalar(x_over[:], xT[:, par], inv_in_scale[:, 0:1], FP8_MAX,
                                  ALU.mult, ALU.min).then_inc(quant_dve, 1)
                dve.wait_ge(quant_dve, 4 * b + 1)
                wait(dve, quant_pool, 2 * (b - 1))
                dve.tensor_scalar(x_clip[:, par], x_over[:], -FP8_MAX, None, ALU.max).then_inc(quant_dve, 1)
                dve.wait_ge(quant_dve, 4 * b + 2)
                dve.tensor_scalar(x_exp[:].bitcast(I32), x_clip[:, par].bitcast(I32), 0x7F800000, None,
                                  ALU.bitwise_and).then_inc(quant_dve, 1)
                dve.wait_ge(quant_dve, 4 * b + 3)
                dve.tensor_scalar(x_big[:, par], x_exp[:], 2.0 ** -6, 1.5 * 2.0 ** 20, ALU.max, ALU.mult).then_inc(quant_dve, 1)

            def maxima(st, b, i):
                half, j = i // 3, i % 3
                dve.wait_ge(ph1_mm, SLOTS * b + i + 1)
                ps = ps2 if st.like == FIRST and i % 2 else ps1
                if j == 0:
                    src, dst = ps[:].rearrange("p (h s) -> p h s", h=HALF), row_max[:, half, 0, :]
                else:
                    src, dst = ps[:].rearrange("p (h s) -> p h s", h=4), row_max[:, half, 1, 4 * j - 4:4 * j]
                dve.tensor_reduce(dst, src, AX_X, ALU.max).then_inc(max_done, 1)

            def negate_and_split(b, half):
                c = 2 * b + half
                at = SLOTS * c
                dve.wait_ge(max_done, SLOTS * b + 3 * half + 3)
                wait(dve, e_ready, c - 1)
                dve.scalar_tensor_tensor(out=neg_max[:, half], in0=row_max[:, half], scalar=-1.0,
                                         in1=neg_floor[:], op0=ALU.mult, op1=ALU.min).then_inc(neg_step, 1)
                dve.wait_ge(neg_step, at + 1)
                wait(dve, max_mm, c - 1)
                dve.tensor_copy(neg_parts[:, half, :, 0, :], neg_max[:, half]).then_inc(neg_step, 1)
                dve.tensor_scalar(e_arg[:, half], neg_max[:, half], MASKED, 0.0, ALU.add, ALU.min).then_inc(neg_step, 1)
                dve.wait_ge(neg_step, at + 2)
                dve.tensor_tensor(neg_r1[:, half], neg_max[:, half], neg_parts[:, half, :, 0, :],
                                  ALU.subtract).then_inc(neg_step, 1)
                dve.wait_ge(neg_step, at + 4)
                dve.tensor_copy(neg_parts[:, half, :, 1, :], neg_r1[:, half]).then_inc(neg_step, 1)
                dve.wait_ge(neg_step, at + 5)
                dve.tensor_tensor(neg_parts[:, half, :, 2, :], neg_r1[:, half], neg_parts[:, half, :, 1, :],
                                  ALU.subtract).then_inc(neg_step, 1)

            def rest1(b, par, qk, bk):
                j = "qk".index(qk)
                dve.wait_ge(part1_ready, 2 * b + j + 1)
                wait(dve, split_ready, 2 * (b - 1) + j + 1)
                for half in range(2):
                    ins = dve.scalar_tensor_tensor(out=rest[qk][:, half, :], in0=bank[bk][:, half * S:half * S + S],
                                                   scalar=bqk_col[:, KT * j + half:KT * j + half + 1],
                                                   in1=parts[qk][:, par, AT[qk][0], half, :], op0=ALU.add, op1=ALU.subtract)
                ins.then_inc(rest_ready, 1)

            def masked_part(b, par, half, bk):
                c = 2 * b + half
                dve.wait_ge(suffix_mm, c + 1)
                dve.wait_ge(e_ready, c + 1)
                wait(dve, norm_step, 3 * (c - 2) + 1)
                dve.tensor_tensor(o_masked[:, half], bank[bk][:, 0:H * NVC].rearrange("p (h d) -> p h d", h=H),
                                  e_sb[:, par, half].rearrange("p t h -> p (t h)").unsqueeze(2).to_broadcast([P, H, NVC]),
                                  ALU.mult).then_inc(masked_ready, 1)

            def sum_o(st, b, half, bk):
                c = 2 * b + half
                dve.wait_ge(o_mm, c + 1)
                dve.wait_ge(masked_ready, c + 1)
                src = ps1[:, 0:512] if st.like == B else bank[bk][:]
                dve.tensor_tensor(o_sum[:, half], src.rearrange("p (h d) -> p h d", h=H)[:, :, 0:NVC],
                                  o_masked[:, half], ALU.add).then_inc(norm_step, 1)

            def divide_o(b, half):
                c = 2 * b + half
                dve.wait_ge(norm_step, 3 * c + 1)
                dve.reciprocal(o_den[:, half, :], o_sum[:, half, :, HD]).then_inc(norm_step, 1)
                dve.wait_ge(norm_step, 3 * c + 2)
                wait(dve, oT_mm, c - 1)
                dve.tensor_tensor(o_tok[:, half].rearrange("p t (h d) -> p (t h) d", d=HD), o_sum[:, half, :, 0:HD],
                                  o_den[:, half].unsqueeze(2).to_broadcast([P, H, HD]),
                                  ALU.mult).then_inc(norm_step, 1)

            def add_up(st, b, par):
                dve.wait_ge(proj_mm, b + 1)
                wait(dve, out_landed[par], 8 * (b - par) + 16)
                src = pso[:, 0] if st.like == B + 1 else bank["A"][:].rearrange("p (t d) -> p t d", t=TB)
                dve.tensor_tensor(y[:, par], src, y1[:, par], ALU.add).then_inc(y_ready, 1)

            def run(st):
                n, p = st.n, st.par
                if st.does("xT") and st.like > 0:
                    normalise(n + 2, p)
                if st.has(-2) and st.like != B:
                    add_up(st, n - 2, p)
                if st.has(1):
                    maxima(st, n + 1, 0)
                if st.does("max_h1"):
                    negate_and_split(n, 1)
                if st.like == 0:
                    dve.wait_ge(w8_mm, 1)
                    dve.tensor_copy(w8T[:], pso[:, 0, 1].bitcast(BF16).rearrange("p (k o) -> p k o", k=KT)).then_inc(w8T_ready, 1)
                    dve.wait_ge(bias_mm, 2)
                    dve.wait_ge(proj_landed, 2 * 16)
                    dve.tensor_tensor(out_bias[:], pso[:, 1, 0], bo_all[:], ALU.add).then_inc(out_bias_ready, 1)
                    clip_x(0, 0)
                if st.has(1):
                    maxima(st, n + 1, 1)
                if st.has(1) and FIRST < st.like < EARLY:
                    clip_x(n + 1, 1 - p)
                if st.does("xT"):
                    rest1(n + 2, p, "q", "B")
                if st.has(1):
                    maxima(st, n + 1, 2)
                if st.like == EARLY:
                    clip_x(n + 1, 1 - p)
                if st.does("xT"):
                    rest1(n + 2, p, "k", "A")
                if st.has(-1):
                    masked_part(n - 1, 1 - p, 1, "B")
                if st.has(1):
                    negate_and_split(n + 1, 0)
                if st.has(-1):
                    sum_o(st, n - 1, 1, "A")
                if st.has(1):
                    maxima(st, n + 1, 3)
                if st.has(-1):
                    divide_o(n - 1, 1)
                if st.like == B:
                    add_up(st, n - 2, p)
                if st.has(0):
                    dve.wait_ge(ffn_mm, n + 1)
                    dve.wait_ge(xb_ready, n + 1)
                    dve.scalar_tensor_tensor(out=y1[:, p], in0=bank["A"][:].rearrange("p (t d) -> p t d", t=TB),
                                             scalar=ffn_scale[:, 0:1], in1=xb[:], op0=ALU.mult, op1=ALU.add).then_inc(y1_ready, 1)
                if st.has(1):
                    maxima(st, n + 1, 4)
                if st.has(0):
                    masked_part(n, p, 0, "B")
                if st.has(1):
                    maxima(st, n + 1, 5)
                if st.like == FIRST:
                    inverse_std(2)
                    normalise(2, 0)
                if st.like == EARLY:
                    negate_and_split(n + 1, 1)
                if st.has(0):
                    sum_o(st, n, 0, "B")
                    divide_o(n, 0)

            for g in range(2):
                dve.wait_ge(x_landed[g], 16)
                link(moments(*X_GROUPS[g]))
                variances(g)
                inverse_std(g)
                normalise(g, g)
                if g == 0:
                    dve.wait_ge(bqk_landed, 16)
                    dve.tensor_copy(bqk_ordered[:].rearrange("m (d h) -> m d h", d=HD),
                                    bqk_row[:].rearrange("m (h d) -> m d h", d=HD)).then_inc(bqk_ready, 1)
            dve.wait_ge(bqk_mm, 1)
            dve.tensor_copy(bqk_col[:], ps1[:, 0:2 * KT]).then_inc(bqk_col_ready, 1)
            scales()
            fp8_weight_fields()
            dve.wait_ge(bqk_col_ready, 1)
            at, last = X_GROUPS[2]
            rest1(0, 0, "q", "B")
            split(dve, 0, 0, "q")
            dve.wait_ge(x_landed[2], 16)
            moments(at, at + 3)
            rest1(0, 0, "k", "A")
            split(dve, 0, 0, "k")
            moments(at + 3, at + 5)
            rest1(1, 1, "q", "B")
            moments(at + 5, at + 8)
            rest1(1, 1, "k", "A")
            fp8_weight()
            dve.wait_ge(bias_mm, 1)
            dve.tensor_copy(bv_T[:], pso[:, 0, 0].rearrange("p (k m) -> p k m", k=KT)).then_inc(bv_T_ready, 1)
            link(moments(at + 8, last))
            variances(2)
            dve.wait_ge(floor_ready, 1)
            all_steps(dve, run)

        @block.tensor
        def _(pe):
            def take(st, bk, name):
                if st is None:
                    before = taken[bk][-1] if taken[bk] else None
                    taken[bk].append((name, sum(who == name for who, _ in taken[bk])))
                else:
                    before = st.use_before(bk, name)
                if before:
                    who, b = before
                    s, per_batch, count = read[who]
                    pe.wait_ge(s, per_batch * b + count)
                return bank[bk]

            taken = {"A": [], "B": []}

            def phase1(st, b, par, i):
                half, j = i // 3, i % 3
                c = SLOTS * b + i
                if st.like == FIRST:
                    ps = (ps1, ps2)[i % 2]
                    wait(pe, max_done, c - 1)
                else:
                    ps = ps1
                    wait(pe, max_done, c)
                if j == 0:
                    pe.wait_ge(stack_landed[half], 16 * STACK_DMAS * (b + 1))
                    for h in range(HALF):
                        hh = HALF * half + h
                        mm = pe.matmul(ps[:, h * P:h * P + P], q_stack[0:K_MAX, par, hh, 0:P],
                                       k_stack[0:K_MAX, par, hh, 0:P], start=True, stop=True)
                else:
                    for h in range(4):
                        hh = HALF * half + 4 * (j - 1) + h
                        pe.matmul(ps[:, h * S:h * S + P], q_stack[0:PROD, par, hh, P:S],
                                  k_stack[0:PROD, par, hh, 0:P], start=True, stop=True)
                        mm = pe.matmul(ps[:, h * S + P:h * S + S], q_stack[0:K_MAX, par, hh, P:S],
                                       k_stack[0:K_MAX, par, hh, P:S], start=True, stop=True)
                mm.then_inc(ph1_mm, 1)

            def phase2(st, b, par, i):
                half, j = i // 3, i % 3
                if st.like == B - 1:
                    ps = (ps2, ps1)[i % 2]
                    pe.wait_ge(max_done, SLOTS * B)
                    if i == 1:
                        pe.wait_ge(max_rows_ready, 2 * B)
                    pe.wait_ge(exp_done, SLOTS * b + max(i - 1, 0))
                else:
                    ps = ps2
                    wait(pe, exp_done, SLOTS * b + i)
                if j == 0:
                    pe.wait_ge(max_landed[half], 16 * (b + 1))
                if j < 2:
                    for h in range(4):
                        hh = HALF * half + 4 * j + h
                        mm = pe.matmul(ps[:, h * S:h * S + S], k_stack[0:K_SOFT, par, hh, 0:P],
                                       q_stack[0:K_SOFT, par, hh, :], start=True, stop=True)
                else:
                    for h in range(HALF):
                        hh = HALF * half + h
                        mm = pe.matmul(ps[:, h * P:h * P + P], k_stack[0:K_SOFT, par, hh, P:S],
                                       q_stack[0:K_SOFT, par, hh, P:S], start=True, stop=True)
                mm.then_inc(ph2_mm, 1)

            def values(st, b, par, i):
                half, j = i // 3, i % 3
                pe.wait_ge(causal_done, SLOTS * b + i + 1)
                if j == 0:
                    wait(pe, o_raw_ready, 2 * (b - 1) + half + 1)
                    if half == 0:
                        pe.wait_ge(v_ready, b + 1)
                    if st.like == 0:
                        pe.wait_ge(w8T_ready, 1)
                        pe.wait_ge(out_bias_ready, 1)
                pr = probs[:, i % 2, :]
                if j < 2:
                    for q in range(4):
                        mm = pe.matmul(pso[32 * q:32 * q + 32, half, j, :], v_sb[:, par, 0, HALF * half + 4 * j + q, :],
                                       pr[:, q * S:q * S + S], start=(j == 0), stop=False, skip_group_check=True)
                else:
                    for g in range(2):
                        for q in range(4):
                            h = 4 * g + q
                            mm = pe.matmul(pso[32 * q:32 * q + 32, half, g, P:S], v_sb[:, par, 1, HALF * half + h, :],
                                           pr[:, h * P:h * P + P], start=False, stop=True, skip_group_check=True)
                mm.then_inc(pv_mm, 1)

            def transpose_x(st, b, par):
                pe.wait_ge(xn_ready, b + 1)
                dst = take(st, "B", "xT")
                for k in range(KT):
                    for t in range(TB):
                        mm = pe.transpose(dst[:, k * S + t * P:k * S + t * P + P], xn[:, par, t, k * P:k * P + P], ident[:])
                mm.then_inc(xT_mm, 1)

            def project_qk(st, b, par, qk, bk):
                j = "qk".index(qk)
                pe.wait_ge(xT_ready, b + 1)
                dst = take(st, bk, qk)
                for m in range(KT):
                    for k in range(KT):
                        col = j * D + m * P
                        mm = pe.matmul(dst[:, m * S:m * S + S], wqk_sb[:, k, col:col + P], xT[:, par, k, :],
                                       start=(k == 0), stop=(k == KT - 1))
                mm.then_inc((q_mm, k_mm)[j], 1)

            def tokens_by(dst, lhsT, rhs):
                for t in range(TB):
                    for k in range(KT):
                        mm = pe.matmul(dst[:, t * D:t * D + D], lhsT[:, k, t * P:t * P + P], rhs[:, k, :],
                                       start=(k == 0), stop=(k == KT - 1))
                return mm

            def project_v(st, b, par):
                pe.wait_ge(xT_ready, b + 1)
                tokens_by(take(st, "B", "v"), xT[:, par], wqkv_sb[:, :, 2 * D:]).then_inc(v_mm, 1)

            def transpose_max(st, b, half, bk):
                pe.wait_ge(neg_step, 6 * (2 * b + half) + 6)
                dst = take(st, bk, f"max_h{half}").ap().bitcast(BF16)
                for t in range(TB):
                    mm = pe.transpose(dst[0:PARTS * HALF, t * P:t * P + P],
                                      neg_parts[:, half, t].rearrange("p r h -> p (r h)"), ident_bf[:])
                mm.then_inc(max_mm, 1)

            def suffix(st, b, par, half):
                pe.wait_ge(v_ready, b + 1)
                dst = take(st, "B", f"suffix{half}")
                heads = slice(HALF * half, HALF * half + HALF)
                w = HALF * NVC
                pe.matmul(dst[:, 0:w], later[:], v_sb[:, par, 0, heads, 0:NVC], start=True, stop=False)
                pe.matmul(dst[:, 0:w], ones[:], v_sb[:, par, 1, heads, 0:NVC], start=False, stop=True)
                pe.matmul(dst[:, w:2 * w], later[:], v_sb[:, par, 1, heads, 0:NVC], start=True, stop=True).then_inc(suffix_mm, 1)

            def transpose_o(st, b, half, bk):
                pe.wait_ge(o_raw_ready, 2 * b + half + 1)
                dst = ps1[:, 0:512] if st.like == B else take(st, bk, f"o{half}")
                for t in range(TB):
                    for g in range(2):
                        at = (2 * t + g) * P
                        mm = pe.transpose(dst[:, at:at + P], o_raw[:, half, g, t * P:t * P + P], ident[:])
                mm.then_inc(o_mm, 1)

            def transpose_norm_o(st, b, half):
                pe.wait_ge(norm_step, 3 * (2 * b + half) + 3)
                dst = (ps1[:, 512:1024], ps2[:, 0:512])[half] if st.like == B else take(st, "A", f"norm_o{half}")
                for t in range(TB):
                    mm = pe.transpose(dst[:, t * P:t * P + P], o_tok[:, half, t, :], ident[:])
                mm.then_inc(oT_mm, 1)

            def project_o(st, b, k):
                pe.wait_ge(oT_ready, 2 * b + k + 1)
                if st.like == B:
                    dst = pso[:, 0].rearrange("p g t -> p (g t)")
                elif k == 0:
                    dst = take(st, "A", "proj")
                else:
                    dst = bank["A"]
                for t in range(TB):
                    mm = pe.matmul(dst[:, t * D:t * D + D], oT[:, 1 - st.par, k, t * P:t * P + P], wo_sb[:, k],
                                   start=(k == 0 and t == 0), stop=(k == KT - 1), skip_group_check=True)
                if k == KT - 1:
                    mm.then_inc(proj_mm, 1)

            def transpose_max_early(b):
                pe.wait_ge(neg_step, 6 * (2 * b + 1) + 6)
                dst = ps1[:].bitcast(BF16)
                for t in range(TB):
                    mm = pe.transpose(dst[0:PARTS * HALF, t * P:t * P + P],
                                      neg_parts[:, 1, t].rearrange("p r h -> p (r h)"), ident_bf[:])
                mm.then_inc(max_mm, 1)

            def bias_product():
                pe.wait_ge(bv_T_ready, 1)
                pe.wait_ge(proj_landed, 2 * 16)
                for k in range(KT):
                    mm = pe.matmul(pso[:, 1, 0], bv_T[:, k], wo_sb[:, k], start=(k == 0), stop=(k == KT - 1))
                mm.then_inc(bias_mm, 1)

            pe.wait_ge(const_ready, 1)
            for _ in range(WARM_UP):
                pe.transpose(ps1[:, 0:P], ident[:], ident[:])
            transpose_x(None, 0, 0)
            pe.wait_ge(bqk_ready, 1)
            pe.transpose(ps1[:, 0:2 * KT], bqk_ordered[:], ident[0:2 * KT, 0:2 * KT]).then_inc(bqk_mm, 1)
            pe.wait_ge(w_ordered, 1)
            for b in range(2):
                if b > 0:
                    transpose_x(None, b, b)
                project_qk(None, b, b, "q", "B")
                project_qk(None, b, b, "k", "A")
            pe.wait_ge(wv_landed, 2 * 16)
            project_v(None, 0, 0)

            for k in range(KT):
                mm = pe.transpose(pso[:, 0, 0, k * P:k * P + P], bv_all[:, k * P:k * P + P], ident[:])
            mm.then_inc(bias_mm, 1)
            pe.wait_ge(w8_ready, 1)
            pe.wait_ge(bv_T_ready, 1)
            for k in range(KT):
                for o in range(KT):
                    mm = pe.transpose(pso[:, 0, 1].bitcast(BF16)[:, k * D + o * P:k * D + o * P + P], w8_bf[:, o, k * P:k * P + P], ident_bf[:])
            mm.then_inc(w8_mm, 1)
            pe.wait_ge(fixed_landed[0], 6 * 16)
            pe.wait_ge(const_ready, CONSTS)

            def last_step(st):
                n, p = st.n, st.par
                before = Step(n - 1, n - 1)
                project_o(before, n - 2, 0)
                values(st, n - 1, 1 - p, SLOTS - 1)
                transpose_norm_o(st, n - 1, 0)
                suffix(st, n - 1, 1 - p, 1)
                transpose_o(st, n - 1, 1, None)
                project_o(before, n - 2, 1)
                project_o(st, n - 1, 0)
                transpose_norm_o(st, n - 1, 1)
                project_o(st, n - 1, 1)

            def run(st):
                n, p = st.n, st.par
                if st.like == B:
                    last_step(st)
                for i in range(SLOTS if st.like < B else 0):
                    if st.has(1):
                        if st.like == 0 and i == 0:
                            pe.wait_ge(fixed_landed[1], 2 * 16)
                        phase1(st, n + 1, 1 - p, i)
                        if st.like == FIRST and i == 1:
                            bias_product()
                        if i == (4 if st.like == FIRST else 5):
                            transpose_max(st, n + 1, 0, "B")
                    if st.has(0) and st.like < B - 1:
                        phase2(st, n, p, i)
                    elif st.has(0):
                        for j in ((0, 1) if i == 0 else (i + 1,) if i + 1 < SLOTS else ()):
                            phase2(st, n, p, j)
                    if i > 0 and st.has(0):
                        values(st, n, p, i - 1)
                    if i == 0 and st.has(-1):
                        values(st, n - 1, 1 - p, SLOTS - 1)
                    if i == 0:
                        if st.has(-1):
                            transpose_norm_o(st, n - 1, 0)
                        if st.does("xT"):
                            transpose_x(st, n + 2, p)
                    elif i == 1:
                        if st.does("max_h1"):
                            transpose_max(st, n, 1, "A")
                        if st.does("xT"):
                            project_qk(st, n + 2, p, "q", "B")
                    elif i == 2:
                        if st.does("xT"):
                            project_qk(st, n + 2, p, "k", "A")
                        if st.has(-1):
                            suffix(st, n - 1, 1 - p, 1)
                    elif i == 3:
                        if st.has(-1):
                            transpose_o(st, n - 1, 1, "A")
                        if st.does("v"):
                            project_v(st, n + 1, 1 - p)
                        if st.has(0):
                            pe.wait_ge(quant_pool, 2 * n + 2)
                            tokens_by(take(st, "A", "ffn"), xq[:, p], w8T[:]).then_inc(ffn_mm, 1)
                    elif i == 4:
                        if st.has(0):
                            suffix(st, n, p, 0)
                        if st.has(-1):
                            transpose_norm_o(st, n - 1, 1)
                    else:
                        if st.has(0):
                            transpose_o(st, n, 0, "B")
                        if st.has(-1) and st.has(1):
                            project_o(st, n - 1, 0)
                            if st.like == EARLY:
                                transpose_max_early(n + 1)
                            project_o(st, n - 1, 1)

            all_steps(pe, run)


_INS = ["L0_attn_x", "L0_attn_Wqkv", "L0_attn_bqkv", "L0_attn_Wo", "L0_attn_bo", "L0_ffn_weight",
        "L0_ffn_weight_scale", "L0_ffn_input_scale"]


def kernel(**inputs):
    import numpy as _np
    import concourse.bacc as _bacc
    from concourse import mybir as _mybir
    from concourse.bass_utils import run_bass_kernel_spmd as _run

    nc = _bacc.Bacc("TRN2", target_bir_lowering=False, num_devices=1)
    arrays, args = {}, []
    for name in _INS:
        a = _np.ascontiguousarray(inputs[name])
        arrays[f"in_{name}_dram"] = a
        args.append(nc.dram_tensor(f"in_{name}_dram", a.shape, _mybir.dt.from_np(a.dtype), kind="ExternalInput").ap())
    args.append(nc.dram_tensor("out_0_dram", (B, S, D), _mybir.dt.float32, kind="ExternalOutput").ap())
    build(nc, *args)
    r = _run(nc, [arrays], core_ids=[0])
    return r.results[0]["out_0_dram"]
```
